# Optimizing a Trainium2 kernel written in Bass

```python
import numpy as np
import jax
import jax.numpy as jnp

def _softmax(x, axis=-1):
    return jax.nn.softmax(x, axis=axis)

def _gelu(x):
    return jax.nn.gelu(x, approximate=True)

def _silu(x):
    return jax.nn.silu(x)

def _sigmoid(x):
    return jax.nn.sigmoid(x)

def _layernorm(x, axis=-1, eps=1e-05):
    m = jnp.mean(x, axis=axis, keepdims=True)
    v = jnp.var(x, axis=axis, keepdims=True)
    return (x - m) / jnp.sqrt(v + eps)

def _scatter_add(tgt, idx, src, axis=0):
    return tgt.at[idx].add(src)

def _segment_sum(src, seg, n):
    return jax.ops.segment_sum(src, seg, n)
kernel_name = 'mk_adj_ffn_d1_adj_r2_ab33bd'

def setup_inputs(seed: int=0):
    np.random.seed(seed)
    _w = jnp.asarray

    def _rec_inputs():
        import jax
        import jax.numpy as jnp
        _gk = jax.random.key(seed)
        x = 7.22e-05 + 1 * jax.random.normal(jax.random.fold_in(_gk, 1), (128, 128, 128), jnp.float32)
        _a = jax.random.bernoulli(jax.random.fold_in(_gk, 2), 0.0625, (128, 128, 128))
        _a = jnp.logical_or(_a, jnp.swapaxes(_a, -1, -2))
        _a = jnp.logical_or(_a, jnp.eye(128, dtype=bool))
        _af = _a.astype(jnp.float32)
        adj = _af
        return (x, adj)
    x, adj = _rec_inputs()

    def _L0_gnn_setup():
        import jax, jax.numpy as jnp
        import numpy as np
        from jax import lax
        DIM = 128
        EPS = 1e-05

        def _bn(h, g, b, m, v):
            scale = g / jnp.sqrt(v + EPS)
            return h * scale[None, :, None] + (b - m * scale)[None, :, None]

        def _conv1d(h, w, pad):
            return lax.conv_general_dilated(h, w, window_strides=(1,), padding=[(pad, pad)], dimension_numbers=('NCH', 'OIH', 'NCH'))
        key = jax.random.key(seed)
        ks = jax.random.split(key, 16)
        bs, n, d = (16, 1024, DIM)
        s = 0.05
        return {'x': jax.random.normal(ks[0], (bs, n, d), jnp.float32), 'mask': jnp.ones((bs, n, n), jnp.float32), 'w_se': jax.random.normal(ks[1], (3, d), jnp.float32) * s, 'b_se': jnp.zeros((3,), jnp.float32), 'conv1_w': jax.random.normal(ks[2], (d, d, 1), jnp.float32) * s, 'bn1_g': jnp.ones((d,), jnp.float32), 'bn1_b': jnp.zeros((d,), jnp.float32), 'bn1_m': jnp.zeros((d,), jnp.float32), 'bn1_v': jnp.ones((d,), jnp.float32), 'conv2_w': jax.random.normal(ks[3], (d, d, 17), jnp.float32) * s, 'bn2_g': jnp.ones((d,), jnp.float32), 'bn2_b': jnp.zeros((d,), jnp.float32), 'bn2_m': jnp.zeros((d,), jnp.float32), 'bn2_v': jnp.ones((d,), jnp.float32), 'w_msg': jax.random.normal(ks[4], (d, d), jnp.float32) * s, 'b_msg': jnp.zeros((d,), jnp.float32), 'w_ih': jax.random.normal(ks[5], (3 * d, 2 * d), jnp.float32) * s, 'b_ih': jnp.zeros((3 * d,), jnp.float32), 'w_hh': jax.random.normal(ks[6], (3 * d, d), jnp.float32) * s, 'b_hh': jnp.zeros((3 * d,), jnp.float32)}
    _L0_gnn_all = _L0_gnn_setup()
    _L0_gnn_in = {k: v for k, v in _L0_gnn_all.items() if k in ('w_se', 'b_se', 'conv1_w', 'bn1_g', 'bn1_b', 'bn1_m', 'bn1_v', 'conv2_w', 'bn2_g', 'bn2_b', 'bn2_m', 'bn2_v', 'w_msg', 'b_msg', 'w_ih', 'b_ih', 'w_hh', 'b_hh')}
    del _L0_gnn_all

    def _L0_ffn_setup():
        import jax, jax.numpy as jnp
        import numpy as np
        B, K, D = (256, 16, 128)
        E = 32
        H = int(D * 0.25)
        key = jax.random.key(seed)
        ks = jax.random.split(key, 7)
        d_rs = D ** (-0.5)
        h_rs = H ** (-0.5)
        x = jax.random.normal(ks[0], (B, K, D), dtype=jnp.float32)
        router_w = jax.random.uniform(ks[1], (E, D), jnp.float32, -d_rs, d_rs)
        router_b = jax.random.uniform(ks[2], (E,), jnp.float32, -d_rs, d_rs)
        W1 = jax.random.uniform(ks[3], (E, D, H), jnp.float32, -h_rs, h_rs)
        b1 = jax.random.uniform(ks[4], (E, H), jnp.float32, -h_rs, h_rs)
        W2 = jax.random.uniform(ks[5], (E, H, D), jnp.float32, -d_rs, d_rs)
        b2 = jax.random.uniform(ks[6], (E, D), jnp.float32, -d_rs, d_rs)
        return {'x': x, 'router_w': router_w, 'router_b': router_b, 'W1': W1, 'b1': b1, 'W2': W2, 'b2': b2}
    _L0_ffn_all = _L0_ffn_setup()
    _L0_ffn_in = {k: v for k, v in _L0_ffn_all.items() if k in ('router_w', 'router_b', 'W1', 'b1', 'W2', 'b2')}
    del _L0_ffn_all
    return {'x': x, 'adj': adj, 'L0_gnn_w_se': _L0_gnn_in['w_se'], 'L0_gnn_b_se': _L0_gnn_in['b_se'], 'L0_gnn_conv1_w': _L0_gnn_in['conv1_w'], 'L0_gnn_bn1_g': _L0_gnn_in['bn1_g'], 'L0_gnn_bn1_b': _L0_gnn_in['bn1_b'], 'L0_gnn_bn1_m': _L0_gnn_in['bn1_m'], 'L0_gnn_bn1_v': _L0_gnn_in['bn1_v'], 'L0_gnn_conv2_w': _L0_gnn_in['conv2_w'], 'L0_gnn_bn2_g': _L0_gnn_in['bn2_g'], 'L0_gnn_bn2_b': _L0_gnn_in['bn2_b'], 'L0_gnn_bn2_m': _L0_gnn_in['bn2_m'], 'L0_gnn_bn2_v': _L0_gnn_in['bn2_v'], 'L0_gnn_w_msg': _L0_gnn_in['w_msg'], 'L0_gnn_b_msg': _L0_gnn_in['b_msg'], 'L0_gnn_w_ih': _L0_gnn_in['w_ih'], 'L0_gnn_b_ih': _L0_gnn_in['b_ih'], 'L0_gnn_w_hh': _L0_gnn_in['w_hh'], 'L0_gnn_b_hh': _L0_gnn_in['b_hh'], 'L0_ffn_router_w': _L0_ffn_in['router_w'], 'L0_ffn_router_b': _L0_ffn_in['router_b'], 'L0_ffn_W1': _L0_ffn_in['W1'], 'L0_ffn_b1': _L0_ffn_in['b1'], 'L0_ffn_W2': _L0_ffn_in['W2'], 'L0_ffn_b2': _L0_ffn_in['b2']}

def reference(x, adj, L0_gnn_w_se, L0_gnn_b_se, L0_gnn_conv1_w, L0_gnn_bn1_g, L0_gnn_bn1_b, L0_gnn_bn1_m, L0_gnn_bn1_v, L0_gnn_conv2_w, L0_gnn_bn2_g, L0_gnn_bn2_b, L0_gnn_bn2_m, L0_gnn_bn2_v, L0_gnn_w_msg, L0_gnn_b_msg, L0_gnn_w_ih, L0_gnn_b_ih, L0_gnn_w_hh, L0_gnn_b_hh, L0_ffn_router_w, L0_ffn_router_b, L0_ffn_W1, L0_ffn_b1, L0_ffn_W2, L0_ffn_b2):
    import jax
    import jax.numpy as jnp

    def _L0_gnn_ref(x, mask, w_se, b_se, conv1_w, bn1_g, bn1_b, bn1_m, bn1_v, conv2_w, bn2_g, bn2_b, bn2_m, bn2_v, w_msg, b_msg, w_ih, b_ih, w_hh, b_hh):
        import jax, jax.numpy as jnp
        import numpy as np
        from jax import lax
        DIM = 128
        EPS = 1e-05

        def _bn(h, g, b, m, v):
            scale = g / jnp.sqrt(v + EPS)
            return h * scale[None, :, None] + (b - m * scale)[None, :, None]

        def _conv1d(h, w, pad):
            return lax.conv_general_dilated(h, w, window_strides=(1,), padding=[(pad, pad)], dimension_numbers=('NCH', 'OIH', 'NCH'))
        d = x.shape[-1]
        xc = jnp.transpose(x, (0, 2, 1))
        h = _bn(_conv1d(xc, conv1_w, 0), bn1_g, bn1_b, bn1_m, bn1_v)
        h = jax.nn.relu(h)
        h = _bn(_conv1d(h, conv2_w, 8), bn2_g, bn2_b, bn2_m, bn2_v)
        x_conv = jnp.transpose(jax.nn.relu(h + xc), (0, 2, 1))
        s = x @ w_se.T + b_se
        sq = jnp.sum(s * s, axis=-1)
        dist = sq[:, :, None] + sq[:, None, :] - 2.0 * jnp.einsum('bnd,bmd->bnm', s, s)
        A = jnp.exp(-dist) * mask
        msg = jax.nn.relu(x @ w_msg.T + b_msg)
        x_nmp = jnp.einsum('bnm,bmd->bnd', A, msg)
        x_in = jnp.concatenate([x_conv, x_nmp], axis=-1)
        gi = x_in @ w_ih.T + b_ih
        gh = x @ w_hh.T + b_hh
        gi_r, gi_z, gi_n = (gi[..., :d], gi[..., d:2 * d], gi[..., 2 * d:])
        gh_r, gh_z, gh_n = (gh[..., :d], gh[..., d:2 * d], gh[..., 2 * d:])
        r = jax.nn.sigmoid(gi_r + gh_r)
        z = jax.nn.sigmoid(gi_z + gh_z)
        nn_ = jnp.tanh(gi_n + r * gh_n)
        return (1.0 - z) * nn_ + z * x

    def _L0_ffn_ref(x, router_w, router_b, W1, b1, W2, b2):
        import jax, jax.numpy as jnp
        import numpy as np
        B, K, D = (256, 16, 128)
        E = 32
        H = int(D * 0.25)
        xf = x.reshape(-1, D)
        logits = xf @ router_w.T + router_b
        idx = jnp.argmax(logits, axis=-1)
        w1t = jnp.take(W1, idx, axis=0)
        h = jnp.einsum('nd,ndh->nh', xf, w1t) + jnp.take(b1, idx, axis=0)
        h = jax.nn.relu(h)
        w2t = jnp.take(W2, idx, axis=0)
        out = jnp.einsum('nh,nhd->nd', h, w2t) + jnp.take(b2, idx, axis=0)
        out = jax.nn.relu(out)
        return out.reshape(x.shape)
    x = x + _L0_gnn_ref(_layernorm(x, axis=-1), adj, L0_gnn_w_se, L0_gnn_b_se, L0_gnn_conv1_w, L0_gnn_bn1_g, L0_gnn_bn1_b, L0_gnn_bn1_m, L0_gnn_bn1_v, L0_gnn_conv2_w, L0_gnn_bn2_g, L0_gnn_bn2_b, L0_gnn_bn2_m, L0_gnn_bn2_v, L0_gnn_w_msg, L0_gnn_b_msg, L0_gnn_w_ih, L0_gnn_b_ih, L0_gnn_w_hh, L0_gnn_b_hh)
    x = x + _L0_ffn_ref(_layernorm(x, axis=-1), L0_ffn_router_w, L0_ffn_router_b, L0_ffn_W1, L0_ffn_b1, L0_ffn_W2, L0_ffn_b2)
    return x

_drawn_inputs = setup_inputs


def setup_inputs(seed=0):
    import zlib

    import numpy as np

    out = dict(_drawn_inputs(seed))
    spreads = {'L0_gnn_b_se': (0.0, 0.8),
     'L0_gnn_bn1_g': (1.0, 0.578),
     'L0_gnn_bn1_b': (0.0, 0.346),
     'L0_gnn_bn1_m': (0.0, 0.322),
     'L0_gnn_bn1_v': (1.0, 0.6),
     'L0_gnn_bn2_g': (1.0, 0.2),
     'L0_gnn_bn2_b': (0.0, 0.45),
     'L0_gnn_bn2_m': (0.0, 0.44),
     'L0_gnn_bn2_v': (1.0, 0.6),
     'L0_gnn_b_msg': (0.0, 0.1),
     'L0_gnn_b_ih': (0.0, 0.1),
     'L0_gnn_b_hh': (0.0, 0.281)}
    factors = {'L0_ffn_b1': 6.365}
    for name, (base, spread) in spreads.items():
        noise = np.random.default_rng([zlib.crc32(name.encode()), seed]).standard_normal(out[name].shape)
        drawn = base * np.exp(spread * noise) if base else spread * noise
        out[name] = jnp.asarray(drawn.astype(out[name].dtype))
    for name, factor in factors.items():
        out[name] = (out[name] * factor).astype(out[name].dtype)
    return out
```

```python
from contextlib import ExitStack

import numpy as np
import concourse.bass as bass
from concourse import mybir

GRAPHS, NODES, D = 128, 128, 128
TAPS = 17
PAD = TAPS // 2
EXPERTS, HID = 32, 32
EPS = 1e-5
QG = 4
QUADS = GRAPHS // QG
TOK = QG * NODES
CHUNKS = EXPERTS * HID // 128
EPC = EXPERTS // CHUNKS
PADDED = NODES + 2 * PAD
NOT_ROUTED = -float(2.0**120)
LOOP_FIRST, LOOP_LAST = 4, 29
VECTORS = 27
W_CONV2, W_CONV1 = 0, TAPS
W_IH_CONV = TAPS + 1
W_IH_NMP = W_IH_CONV + 3
W_HH = W_IH_NMP + 3
W_MSG = W_HH + 3
W_SMALL = W_MSG + 1
ROUTER_COL = W_SMALL * 128
SE_COL = ROUTER_COL + EXPERTS
SE_ROWS = 67
WT_COLS = SE_COL + SE_ROWS


class Quad:

    def __init__(self, n, it=None):
        self.n, self.it, self.par = n, it, n % 2

    def __add__(self, k):
        return Quad(self.n + k, self.it)

    def exists(self):
        return self.it is not None or 0 <= self.n < QUADS

    def index(self):
        return self.n if self.it is None else 2 * self.it + self.n

    def events(self):
        return self.n + 1 if self.it is None else 2 * self.it + (self.n + 1)

    def loads(self):
        n = self.n // 2 + 1
        return 16 * n if self.it is None else 16 * self.it + 16 * n


def wait_quad(eng, sem, q):
    if q.n >= 0:
        eng.wait_ge(sem, q.events())


def pass_quad(eng, sem, q, passed):
    if q.n >= 0:
        eng.wait_ge(sem, q.events())
        eng.sem_inc(passed, 1)


def wait_dma(eng, sems, q):
    if q.n >= 0:
        eng.wait_ge(sems[q.par], q.loads())


def run_steps(eng, step):
    for n in range(-1, LOOP_FIRST):
        step(Quad(n))
    with eng.Fori(0, (LOOP_LAST - LOOP_FIRST + 1) // 2) as it:
        for k in range(2):
            step(Quad(LOOP_FIRST + k, it))
    for n in range(LOOP_LAST + 1, QUADS + 2):
        step(Quad(n))


def program(nc, a, out):
    f32, f32r, bf16, i32 = mybir.dt.float32, mybir.dt.float32r, mybir.dt.bfloat16, mybir.dt.int32
    ALU, ACT, AX = mybir.AluOpType, mybir.ActivationFunctionType, mybir.AxisListType
    ctx = ExitStack()

    def sb(name, shape, dt=f32):
        return ctx.enter_context(nc.sbuf_tensor(name, shape, dt))

    def sem(name):
        return ctx.enter_context(nc.semaphore(name))

    def sems(name, n):
        return [sem(f"{name}{i}") for i in range(n)]

    with ctx:
        x_v = a["x"].rearrange("(q g) t d -> q t g d", g=QG)
        adj_v = a["adj"].rearrange("(q g) t d -> q t g d", g=QG)
        out_v = out.rearrange("(q g) t d -> q t g d", g=QG)

        wt_hi = sb("wt_hi", [128, WT_COLS], f32r)
        wt_lo = sb("wt_lo", [128, WT_COLS], f32r)
        wmsg = sb("wmsg", [128, 128])
        w1_hi = sb("w1_hi", [128, EXPERTS * HID], f32r)
        w1_lo = sb("w1_lo", [128, EXPERTS * HID], f32r)
        w2_hi = sb("w2_hi", [128, CHUNKS, 128], f32r)
        w2_lo = sb("w2_lo", [128, CHUNKS, 128], f32r)
        b1_or_off = sb("b1_or_off", [96, EXPERTS * HID], bf16)
        b2_parts = sb("b2_parts", [96, 128], bf16)
        bmsg_parts = sb("bmsg_parts", [65, 128], bf16)
        ones_bf = sb("ones_bf", [65, 128], bf16)
        ident = sb("ident", [128, 128])
        ident_bf = sb("ident_bf", [128, 128], bf16)
        rank = sb("rank", [128, EXPERTS])
        minus_half = sb("minus_half", [128, QG])
        (V_G1, V_B1, V_M1, V_V1, V_G2, V_B2, V_M2, V_V2, V_IHR, V_IHZ, V_IHN, V_HHR, V_HHZ, V_HHN,
         V_S1, V_S2, V_T1, V_T2, V_HR, V_HZ, V_HN) = range(21)
        vec = sb("vec", [128, 24])
        bse = sb("bse", [SE_ROWS, 1])
        brout = sb("brout", [EXPERTS, 1])

        x_nat = sb("x_nat", [128, 2, QG, D])
        adj_nat = sb("adj_nat", [128, 2, QG, NODES])
        xn = sb("xn", [128, 2, QG, D])
        xnT = sb("xnT", [128, 2, TOK])
        xnT_hi = sb("xnT_hi", [128, 2, TOK], f32r)
        xnT_lo = sb("xnT_lo", [128, 2, TOK], f32r)
        adjT = sb("adjT", [128, 2, TOK])
        h1 = sb("h1", [128, 2, TOK])
        h1_hi = sb("h1_hi", [128, 2, QG, PADDED], f32r)
        h1_lo = sb("h1_lo", [128, 2, QG, PADDED], f32r)
        dist_l = sb("dist_l", [SE_ROWS, 2, TOK])
        dist_r = sb("dist_r", [SE_ROWS, 2, TOK])
        msg = sb("msg", [128, 2, TOK])
        att = sb("att", [128, 2, TOK])
        nmp_hi = sb("nmp_hi", [128, 2, TOK], f32r)
        nmp_lo = sb("nmp_lo", [128, 2, TOK], f32r)
        xc_hi = sb("xc_hi", [128, 2, TOK], f32r)
        xc_lo = sb("xc_lo", [128, 2, TOK], f32r)
        x2 = sb("x2", [128, 2, QG, D])
        yn = sb("yn", [128, 2, QG, D])
        yn_hi = sb("yn_hi", [128, 2, TOK], f32r)
        yn_lo = sb("yn_lo", [128, 2, TOK], f32r)
        y = sb("y", [128, 2, QG, D])
        hid_hi = sb("hid_hi", [128, 4, TOK], f32r)
        hid_lo = sb("hid_lo", [128, 4, TOK], f32r)
        work = sb("work", [128, 10, TOK])
        (E_, T_, GH, TR, TZ, W_, N_, DE, F_, O_) = range(10)
        logitT = sb("logitT", [EXPERTS, TOK])
        lmax = sb("lmax", [128, QG])
        ranked = sb("ranked", [128, QG, EXPERTS])
        first = sb("first", [128, QG])
        onehot = sb("onehot", [128, QG, 3, EXPERTS], bf16)
        onehotT = sb("onehotT", [96, 2, TOK], bf16)
        stats = sb("stats", [128, 2, QG, 6])
        mv = sb("mv", [128, 2, QG, 2])
        negm = sb("negm", [128, 4, QG])
        veps = sb("veps", [128, 4, QG])
        rstd = sb("rstd", [128, 4, QG])

        flat = work[:, :, :].rearrange("p a n -> p (a n)")
        c2_raw = flat[:, 0:2176]
        ih_raw = flat[:, 2176:2944]
        hh_raw = flat[:, 2944:3328]
        c1_raw = flat[:, 3328:3456]
        msg_raw = flat[:, 3456:3584]
        rout_raw = flat[0:EXPERTS, 3584:3712]
        se_raw = flat[0:SE_ROWS, 3712:3840]
        w1_raw = flat[:, 3840:4864]
        w2_raw = y[:, :, :, :].rearrange("p a g d -> p (a g d)")
        hflat = h1[:, :, :].rearrange("p a n -> p (a n)")
        b1_raw = hflat[0:96, 0:32]
        b1_rest = hflat[0:96, 32:64]
        b2_raw = hflat[0:96, 64:192]
        b2_rest = hflat[0:96, 192:320]
        bm_raw = hflat[0:65, 320:448]
        bm_rest = hflat[0:65, 448:576]
        b1_wide = att[0:96, :, :].rearrange("p a n -> p (a n)")
        b1_p = sb("b1_p", [96, HID], bf16)
        b2_p = sb("b2_p", [96, 128], bf16)
        bm_p = sb("bm_p", [65, 128], bf16)
        rank_i = sb("rank_i", [128, EXPERTS], i32)

        bank = [ctx.enter_context(nc.psum_tensor(f"bank{i}", [128, TOK], f32)) for i in range(8)]
        b1_bf = bank[1][:, :].bitcast(bf16)

        x_loaded, adj_loaded, stored = sems("x_loaded", 2), sems("adj_loaded", 2), sems("stored", 2)
        w_loaded, v_loaded, f_loaded = sem("w_loaded"), sem("v_loaded"), sem("f_loaded")
        zeroed, consts, pool_setup, bn_pow, bn_vec, bn_scaled = (sem(n) for n in (
            "zeroed", "consts", "pool_setup", "bn_pow", "bn_vec", "bn_scaled"))
        bias_split, bias_wide, w_turned, w_hi, w_lo, f_split = (sem(n) for n in (
            "bias_split", "bias_wide", "w_turned", "w_hi_done", "w_lo_done", "f_split"))
        (ln1_stats, ln1_mv, ln1_nv, ln1_rstd, xn_ready, xnT_done, xnT_full, xnT_hi_ok, xnT_lo_ok,
         adjT_done, adjT_ok, conv1_done, h1_full, h1_hi_ok, h1_lo_ok, se_done, se_sq, se_l, msg_done,
         msg_ok, dist_done, exp_ok, att_ok, nmp_done, nmp_hi_ok, nmp_lo_ok, conv2_done, xc_t, xc_hi_ok,
         xc_lo_ok, gate_n_h, gate_r, gate_z, gate_n_i, gh_ok, tr_ok, tz_ok, rgh_ok, w_ok, n_ok, gru_d,
         gru_e, gru_f, gruT_done, x2_ok, ln2_stats, ln2_mv, ln2_nv, ln2_rstd, yn_ready, ynT_done,
         yn_hi_ok, yn_lo_ok, router_done, logitT_ok, logit_done, am_max, am_eq, am_rank, am_first,
         onehot_ok, onehotT_done, onehotT_ok, o_ok, ffnT_done, y_ok) = (
            sem(n) for n in """ln1_stats ln1_mv ln1_nv ln1_rstd xn_ready xnT_done xnT_full xnT_hi_ok
            xnT_lo_ok adjT_done adjT_ok conv1_done h1_full h1_hi_ok h1_lo_ok se_done se_sq se_l msg_done
            msg_ok dist_done exp_ok att_ok nmp_done nmp_hi_ok nmp_lo_ok conv2_done xc_t xc_hi_ok
            xc_lo_ok gate_n_h gate_r gate_z gate_n_i gh_ok tr_ok tz_ok rgh_ok w_ok n_ok gru_d gru_e
            gru_f gruT_done x2_ok ln2_stats ln2_mv ln2_nv ln2_rstd yn_ready ynT_done yn_hi_ok yn_lo_ok
            router_done logitT_ok logit_done am_max am_eq am_rank am_first onehot_ok onehotT_done
            onehotT_ok o_ok ffnT_done y_ok""".split())
        dve_passed, pool_passed, pe_passed = sem("dve_passed"), sem("pool_passed"), sem("pe_passed")
        w1_done, w2_done = sems("w1_done", CHUNKS), sems("w2_done", CHUNKS)
        hid_hi_ok, hid_lo_ok = sems("hid_hi_ok", CHUNKS), sems("hid_lo_ok", CHUNKS)

        HBANK = [0, 1, 3, 2]

        def f(ap):
            return ap.bitcast(f32)

        block = ctx.enter_context(nc.Block())

        @block.sync
        def _(sp):
            sp.dma_start(c2_raw, a["L0_gnn_conv2_w"].rearrange("o i k -> o (i k)")).then_inc(w_loaded, 16)
            sp.dma_start(c1_raw, a["L0_gnn_conv1_w"].rearrange("o i k -> o (i k)")).then_inc(w_loaded, 16)
            sp.dma_start(ih_raw.rearrange("p (g c) -> p g c", g=3),
                         a["L0_gnn_w_ih"].rearrange("(g o) c -> o g c", g=3)).then_inc(w_loaded, 16)
            sp.dma_start(hh_raw.rearrange("p (g c) -> p g c", g=3),
                         a["L0_gnn_w_hh"].rearrange("(g o) c -> o g c", g=3)).then_inc(w_loaded, 16)
            sp.dma_start(msg_raw, a["L0_gnn_w_msg"]).then_inc(w_loaded, 16)
            sp.dma_start(rout_raw, a["L0_ffn_router_w"]).then_inc(w_loaded, 16)
            sp.wait_ge(zeroed, 1)
            for r in (0, 32, 64):
                sp.dma_start(se_raw[r:r + 3, :], a["L0_gnn_w_se"]).then_inc(w_loaded, 16)
            sp.dma_start(w1_raw.rearrange("p (e h) -> p e h", e=EXPERTS),
                         a["L0_ffn_W1"].rearrange("e d h -> d e h")).then_inc(f_loaded, 16)
            sp.dma_start(w2_raw.rearrange("p (c d) -> p c d", c=CHUNKS),
                         a["L0_ffn_W2"].rearrange("(c e) h d -> (e h) c d", c=CHUNKS)).then_inc(f_loaded, 16)

            def step(q):
                front, back = q + 1, q + (-2)
                if front.exists():
                    wait_quad(sp, x2_ok, front + (-2))
                    sp.dma_start(x_nat[:, front.par, :, :], x_v[bass.ds(front.index(), 1)][0]
                                 ).then_inc(x_loaded[front.par], 16)
                    wait_quad(sp, adjT_done, front + (-2))
                    sp.dma_start(adj_nat[:, front.par, :, :], adj_v[bass.ds(front.index(), 1)][0]
                                 ).then_inc(adj_loaded[front.par], 16)
                if back.exists():
                    wait_quad(sp, y_ok, back)
                    sp.dma_start(out_v[bass.ds(back.index(), 1)][0], y[:, back.par, :, :]
                                 ).then_inc(stored[back.par], 16)

            run_steps(sp, step)
            wait_dma(sp, stored, Quad(QUADS - 2))
            wait_dma(sp, stored, Quad(QUADS - 1))

        @block.gpsimd
        def _(pool):
            done_ops = [0]

            def link(ins):
                done_ops[0] += 1
                ins.then_inc(pool_setup, 1)
                pool.wait_ge(pool_setup, done_ops[0])

            link(pool.memset(se_raw, 0.0))
            link(pool.memset(bm_raw, 0.0))
            pool.sem_inc(zeroed, 1)
            link(pool.memset(ident[:], 0.0))
            link(pool.affine_select(out=ident[:], in_=ident[:], compare_op=ALU.not_equal, fill=1.0, base=0,
                                    pattern=[[-1, 128]], channel_multiplier=1))
            link(pool.memset(minus_half[:], -0.5))
            link(pool.memset(ones_bf[:], 1.0))
            link(pool.memset(ident_bf[:], 0.0))
            link(pool.affine_select(out=ident_bf[:], in_=ident_bf[:], compare_op=ALU.not_equal, fill=1.0, base=0,
                                    pattern=[[-1, 128]], channel_multiplier=1))
            pool.wait_ge(bn_vec, 1)
            link(pool.tensor_tensor(vec[:, V_V1:V_V1 + 1], vec[:, V_V1:V_V1 + 1], minus_half[:, 0:1], ALU.pow))
            pool.tensor_tensor(vec[:, V_V2:V_V2 + 1], vec[:, V_V2:V_V2 + 1], minus_half[:, 0:1], ALU.pow
                               ).then_inc(bn_pow, 1)
            pool.wait_ge(bn_pow, 1)
            link(pool.memset(f(h1_hi[:]).rearrange("p a g n -> p (a g n)"), 0.0))
            link(pool.memset(f(h1_lo[:]).rearrange("p a g n -> p (a g n)"), 0.0))
            link(pool.memset(dist_l[:], 0.0))
            link(pool.memset(dist_r[:], 0.0))
            link(pool.iota(rank_i[:], pattern=[[-1, EXPERTS]], base=EXPERTS, channel_multiplier=0))
            link(pool.tensor_copy(rank[:], rank_i[:]))
            link(pool.memset(dist_l[32:35, :, :], -0.5))
            link(pool.memset(dist_r[64:67, :, :], -0.5))
            pool.wait_ge(bias_wide, 1)
            for r, fill in ((0, NOT_ROUTED), (32, 0.0), (64, 0.0)):
                rows = b1_wide[r:r + 32, :].rearrange("p (e h) -> p e h", h=HID)
                link(pool.affine_select(out=rows, in_=rows, compare_op=ALU.is_equal, fill=fill, base=0,
                                        pattern=[[-1, EXPERTS], [0, HID]], channel_multiplier=1))
            pool.tensor_copy(b1_or_off[:], b1_wide).then_inc(consts, 1)
            pool.wait_ge(consts, 1)

            def rstd_and_normalize(q, k, nv, rstd_ok, src, dst, done):
                p = q.par
                wait_quad(pool, nv, q)
                pool.tensor_tensor(rstd[:, k + p, :], veps[:, k + p, :], minus_half[:], ALU.pow
                                   ).then_inc(rstd_ok, 1)
                pass_quad(pool, rstd_ok, q, pool_passed)
                for g in range(QG):
                    last = pool.tensor_scalar(dst[:, p, g, :], src[:, p, g, :], negm[:, k + p, g:g + 1],
                                              rstd[:, k + p, g:g + 1], ALU.add, ALU.mult)
                last.then_inc(done, 1)

            def step(q):
                front = q + 1
                if front.exists():
                    p = front.par
                    wait_quad(pool, xnT_done, front + (-2))
                    rstd_and_normalize(front, 0, ln1_nv, ln1_rstd, x_nat, xn, xn_ready)
                    wait_quad(pool, xnT_hi_ok, front)
                    pool.tensor_tensor(xnT_lo[:, p, :], xnT[:, p, :], f(xnT_hi[:, p, :]), ALU.subtract
                                       ).then_inc(xnT_lo_ok, 1)
                    wait_quad(pool, h1_hi_ok, front)
                    pool.tensor_tensor(h1_lo[:, p, :, PAD:PAD + NODES],
                                       h1[:, p, :].rearrange("p (g t) -> p g t", g=QG),
                                       f(h1_hi[:, p, :, PAD:PAD + NODES]), ALU.subtract).then_inc(h1_lo_ok, 1)
                if q.exists():
                    wait_quad(pool, n_ok, q)
                    pool.tensor_tensor(work[:, DE, :], xnT[:, q.par, :], work[:, N_, :], ALU.subtract
                                       ).then_inc(gru_d, 1)
                if front.exists():
                    wait_quad(pool, exp_ok, front)
                    wait_quad(pool, adjT_ok, front)
                    wait_quad(pool, nmp_done, front + (-2))
                    pool.tensor_tensor(att[:, p, :], work[:, E_, :], adjT[:, p, :], ALU.mult
                                       ).then_inc(att_ok, 1)
                if q.exists():
                    wait_quad(pool, ynT_done, q + (-2))
                    rstd_and_normalize(q, 2, ln2_nv, ln2_rstd, x2, yn, yn_ready)

            run_steps(pool, step)

        @block.scalar
        def _(act):
            for col, name in ((V_G1, "bn1_g"), (V_B1, "bn1_b"), (V_M1, "bn1_m"), (V_V1, "bn1_v"),
                              (V_G2, "bn2_g"), (V_B2, "bn2_b"), (V_M2, "bn2_m"), (V_V2, "bn2_v")):
                act.dma_start(vec[:, col:col + 1], a["L0_gnn_" + name].rearrange("(p o) -> p o", o=1)
                              ).then_inc(v_loaded, 16)
            for col, name in ((V_IHR, "b_ih"), (V_HHR, "b_hh")):
                for g in range(3):
                    act.dma_start(vec[:, col + g:col + g + 1],
                                  a["L0_gnn_" + name][g * 128:g * 128 + 128].rearrange("(p o) -> p o", o=1)
                                  ).then_inc(v_loaded, 16)
            for r in (0, 32, 64):
                act.dma_start(bse[r:r + 3, :], a["L0_gnn_b_se"].rearrange("(p o) -> p o", o=1)
                              ).then_inc(v_loaded, 16)
            act.dma_start(brout[:], a["L0_ffn_router_b"].rearrange("(p o) -> p o", o=1)).then_inc(v_loaded, 16)
            act.wait_ge(zeroed, 1)
            for r in (0, 32, 64):
                act.dma_start(b1_raw[r:r + 32, :], a["L0_ffn_b1"]).then_inc(v_loaded, 16)
                act.dma_start(b2_raw[r:r + 32, :], a["L0_ffn_b2"]).then_inc(v_loaded, 16)
                act.dma_start(bm_raw[r:r + 1, :], a["L0_gnn_b_msg"].rearrange("(o p) -> o p", o=1)
                              ).then_inc(v_loaded, 16)
            for g in range(8):
                act.wait_ge(w_turned, g + 1)
                lo, hi = g * 512, min(g * 512 + 512, WT_COLS)
                if g == W_MSG // 4:
                    k = (W_MSG % 4) * 128
                    act.activation(wmsg[:], bank[g][:, k:k + 128], ACT.Copy)
                act.activation(wt_hi[:, lo:hi], bank[g][:, 0:hi - lo], ACT.Copy).then_inc(w_hi, 1)
            act.wait_ge(v_loaded, 16 * VECTORS)
            act.wait_ge(bn_vec, 3)

            def step(q):
                front, back = q + 1, q + (-1)
                if back.exists():
                    p = back.par
                    wait_quad(act, ynT_done, back)
                    wait_quad(act, w2_done[CHUNKS - 1], back + (-2))
                    act.activation(yn_hi[:, p, :], bank[1][:], ACT.Copy).then_inc(yn_hi_ok, 1)
                    wait_quad(act, router_done, back)
                    wait_quad(act, logit_done, back + (-1))
                    act.activation(logitT[:], bank[2][0:EXPERTS, :], ACT.Identity, bias=brout[:]
                                   ).then_inc(logitT_ok, 1)
                if front.exists():
                    p = front.par
                    wait_quad(act, xnT_done, front)
                    wait_quad(act, gru_d, front + (-2))
                    act.activation(xnT[:, p, :], bank[2][:], ACT.Copy).then_inc(xnT_full, 1)
                    wait_quad(act, adjT_done, front)
                    wait_quad(act, att_ok, front + (-2))
                    act.activation(adjT[:, p, :], bank[3][:], ACT.Copy).then_inc(adjT_ok, 1)
                if q.exists():
                    wait_quad(act, xc_t, q)
                    wait_quad(act, gate_n_i, q + (-2))
                    act.activation(xc_hi[:, q.par, :], work[:, T_, :], ACT.Relu).then_inc(xc_hi_ok, 1)
                    wait_quad(act, gate_n_h, q)
                    wait_quad(act, rgh_ok, q + (-1))
                    act.activation(work[:, GH, :], bank[7][:], ACT.Identity, bias=vec[:, V_HN:V_HN + 1],
                                   scale=0.5).then_inc(gh_ok, 1)
                if front.exists():
                    p = front.par
                    wait_quad(act, conv1_done, front)
                    wait_quad(act, h1_lo_ok, front + (-2))
                    act.activation(h1[:, p, :], bank[2][:], ACT.Relu, bias=vec[:, V_T1:V_T1 + 1]
                                   ).then_inc(h1_full, 1)
                    wait_quad(act, se_done, front)
                    wait_quad(act, dist_done, front + (-2))
                    act.activation(dist_r[0:3, p, :], bank[3][0:3, :], ACT.Identity, bias=bse[0:3, :])
                    act.activation(dist_r[32:35, p, :], bank[3][32:35, :], ACT.Square, bias=bse[32:35, :])
                    act.activation(dist_l[64:67, p, :], bank[3][64:67, :], ACT.Square, bias=bse[64:67, :]
                                   ).then_inc(se_sq, 1)
                if q.exists():
                    wait_quad(act, gate_r, q)
                    act.activation(work[:, TR, :], bank[4][:], ACT.Tanh, bias=vec[:, V_HR:V_HR + 1],
                                   scale=0.5).then_inc(tr_ok, 1)
                    wait_quad(act, gate_z, q)
                    wait_quad(act, gru_e, q + (-1))
                    act.activation(work[:, TZ, :], bank[5][:], ACT.Tanh, bias=vec[:, V_HZ:V_HZ + 1],
                                   scale=0.5).then_inc(tz_ok, 1)
                if front.exists():
                    wait_quad(act, msg_done, front)
                    wait_quad(act, nmp_done, front + (-2))
                    act.activation(msg[:, p, :], bank[0][:], ACT.Relu).then_inc(msg_ok, 1)
                if q.exists():
                    wait_quad(act, w_ok, q)
                    wait_quad(act, gru_f, q + (-1))
                    act.activation(work[:, N_, :], work[:, W_, :], ACT.Tanh, bias=vec[:, V_IHN:V_IHN + 1]
                                   ).then_inc(n_ok, 1)
                if front.exists():
                    wait_quad(act, dist_done, front)
                    wait_quad(act, att_ok, front + (-1))
                    act.activation(work[:, E_, :], bank[2][:], ACT.Exp, scale=2.0).then_inc(exp_ok, 1)

                def hidden(c):
                    wait_quad(act, w1_done[c], back)
                    wait_quad(act, w2_done[(c + 4) % CHUNKS], back if c >= 4 else back + (-1))
                    act.activation(hid_hi[:, c % 4, :], bank[4 + HBANK[c % 4]][:], ACT.Relu
                                   ).then_inc(hid_hi_ok[c], 1)

                if back.exists():
                    for c in range(5):
                        hidden(c)
                if front.exists():
                    wait_quad(act, nmp_done, front)
                    wait_quad(act, gate_n_i, front + (-2))
                    act.activation(nmp_hi[:, p, :], bank[2][:], ACT.Copy).then_inc(nmp_hi_ok, 1)
                if back.exists():
                    for c in range(5, CHUNKS):
                        hidden(c)
                    wait_quad(act, w2_done[CHUNKS - 1], back)
                    wait_quad(act, ffnT_done, back + (-1))
                    act.activation(work[:, O_, :], bank[1][:], ACT.Relu).then_inc(o_ok, 1)

            run_steps(act, step)

        @block.vector
        def _(dve):
            dve.wait_ge(v_loaded, 16 * VECTORS)
            dve.tensor_scalar(vec[:, V_V1:V_V1 + 1], vec[:, V_V1:V_V1 + 1], EPS, None, ALU.add)
            dve.tensor_scalar(vec[:, V_V2:V_V2 + 1], vec[:, V_V2:V_V2 + 1], EPS, None, ALU.add).then_inc(bn_vec, 1)
            chain = [0]

            def link(ins):
                chain[0] += 1
                ins.then_inc(bias_split, 1)
                dve.wait_ge(bias_split, chain[0])

            def parts(raw, rest, part, dst, groups, rows):
                src = raw
                for k, r in enumerate(groups):
                    link(dve.tensor_copy(part, src))
                    link(dve.tensor_copy(dst[r:r + rows], part[r:r + rows]))
                    if k < 2:
                        link(dve.tensor_tensor(rest, src, part, ALU.subtract))
                        src = rest

            parts(b2_raw, b2_rest, b2_p[:], b2_parts[:], (0, 32, 64), 32)
            link(dve.memset(bmsg_parts[:], 0.0))
            parts(bm_raw, bm_rest, bm_p[:], bmsg_parts[:], (0, 32, 64), 1)
            parts(b1_raw, b1_rest, b1_p[:], b1_wide.rearrange("p (e h) -> p e h", h=HID)[:, 0, :],
                  (0, 32, 64), 32)
            link(dve.tensor_copy(b1_rest, b1_wide[:, 0:HID]))
            dve.tensor_copy(b1_wide.rearrange("p (e h) -> p e h", h=HID),
                            b1_rest.rearrange("p (e h) -> p e h", e=1).to_broadcast([96, EXPERTS, HID])
                            ).then_inc(bias_wide, 1)
            dve.wait_ge(bn_pow, 1)
            for s, g, v, m, b, t in ((V_S1, V_G1, V_V1, V_M1, V_B1, V_T1), (V_S2, V_G2, V_V2, V_M2, V_B2, V_T2)):
                link(dve.tensor_tensor(vec[:, s:s + 1], vec[:, g:g + 1], vec[:, v:v + 1], ALU.mult))
                link(dve.tensor_tensor(vec[:, t:t + 1], vec[:, m:m + 1], vec[:, s:s + 1], ALU.mult))
                link(dve.tensor_tensor(vec[:, t:t + 1], vec[:, b:b + 1], vec[:, t:t + 1], ALU.subtract))
            link(dve.tensor_tensor(vec[:, V_HR:V_HR + 2], vec[:, V_IHR:V_IHR + 2], vec[:, V_HHR:V_HHR + 2], ALU.add))
            dve.tensor_scalar(vec[:, V_HR:V_HR + 2], vec[:, V_HR:V_HR + 2], 0.5, None, ALU.mult)
            dve.tensor_scalar(vec[:, V_HN:V_HN + 1], vec[:, V_HHN:V_HHN + 1], 0.5, None, ALU.mult
                              ).then_inc(bn_vec, 1)
            dve.wait_ge(w_loaded, 16 * 9)
            dve.tensor_scalar(c2_raw, c2_raw, vec[:, V_S2:V_S2 + 1], None, ALU.mult)
            dve.tensor_scalar(c1_raw, c1_raw, vec[:, V_S1:V_S1 + 1], None, ALU.mult).then_inc(bn_scaled, 1)
            dve.wait_ge(bn_scaled, 1)
            dve.tensor_copy(vec[:, 23:24], vec[:, V_S1:V_S1 + 1]).then_inc(bn_vec, 1)
            for g in range(8):
                dve.wait_ge(w_hi, g + 1)
                lo, hi = g * 512, min(g * 512 + 512, WT_COLS)
                dve.tensor_tensor(wt_lo[:, lo:hi], bank[g][:, 0:hi - lo], f(wt_hi[:, lo:hi]), ALU.subtract
                                  ).then_inc(w_lo, 1)
            dve.wait_ge(f_loaded, 32)
            w2h, w2l = (t[:].rearrange("p c d -> p (c d)") for t in (w2_hi, w2_lo))
            dve.tensor_copy(w1_hi[:], w1_raw)
            dve.tensor_copy(w2h, w2_raw).then_inc(f_split, 1)
            dve.wait_ge(f_split, 1)
            dve.tensor_tensor(w1_lo[:], w1_raw, f(w1_hi[:]), ALU.subtract)
            dve.tensor_tensor(w2l, w2_raw, f(w2h), ALU.subtract).then_inc(f_split, 1)
            dve.wait_ge(f_split, 2)

            def layer_stats(q, k, src, stats_ok, mv_ok, nv_ok):
                p = q.par
                for g in range(QG):
                    last = dve.bn_stats(stats[:, p, g, :], src[:, p, g, :])
                last.then_inc(stats_ok, 1)
                pass_quad(dve, stats_ok, q, dve_passed)
                for g in range(QG):
                    last = dve.bn_aggr(mv[:, p, g, :], stats[:, p, g, :])
                last.then_inc(mv_ok, 1)
                wait_quad(dve, mv_ok, q)
                dve.tensor_scalar(negm[:, k + p, :], mv[:, p, :, 0], -1.0, None, ALU.mult)
                dve.tensor_scalar(veps[:, k + p, :], mv[:, p, :, 1], EPS, None, ALU.add).then_inc(nv_ok, 1)

            def step(q):
                front, back, last_ = q + 1, q + (-1), q + (-2)
                if last_.exists():
                    p = last_.par
                    wait_quad(dve, ffnT_done, last_)
                    wait_dma(dve, stored, last_ + (-2))
                    dve.tensor_tensor(y[:, p, :, :], bank[3][:].rearrange("p (g d) -> p g d", g=QG),
                                      x2[:, p, :, :], ALU.add).then_inc(y_ok, 1)
                if back.exists():
                    p = back.par
                    wait_quad(dve, yn_hi_ok, back)
                    dve.tensor_tensor(yn_lo[:, p, :], bank[1][:], f(yn_hi[:, p, :]), ALU.subtract
                                      ).then_inc(yn_lo_ok, 1)
                if front.exists():
                    wait_dma(dve, x_loaded, front)
                    layer_stats(front, 0, x_nat, ln1_stats, ln1_mv, ln1_nv)
                if back.exists():
                    logit = bank[1][:, 0:QG * EXPERTS].rearrange("p (g e) -> p g e", g=QG)
                    wait_quad(dve, logit_done, back)
                    dve.tensor_reduce(lmax[:], logit, AX.X, ALU.max).then_inc(am_max, 1)
                    wait_quad(dve, am_max, back)
                    dve.tensor_tensor(ranked[:], logit, lmax[:].rearrange("p (g o) -> p g o", o=1)
                                      .to_broadcast([128, QG, EXPERTS]), ALU.is_equal).then_inc(am_eq, 1)
                    wait_quad(dve, am_eq, back)
                    dve.tensor_tensor(ranked[:], ranked[:], rank[:].rearrange("p (o e) -> p o e", o=1)
                                      .to_broadcast([128, QG, EXPERTS]), ALU.mult).then_inc(am_rank, 1)
                    wait_quad(dve, am_rank, back)
                    dve.tensor_reduce(first[:], ranked[:], AX.X, ALU.max).then_inc(am_first, 1)
                    wait_quad(dve, am_first, back)
                    wait_quad(dve, onehotT_done, back + (-1))
                    dve.tensor_tensor(onehot[:], ranked[:].rearrange("p g (o e) -> p g o e", o=1)
                                      .to_broadcast([128, QG, 3, EXPERTS]),
                                      first[:].rearrange("p (g o e) -> p g o e", o=1, e=1)
                                      .to_broadcast([128, QG, 3, EXPERTS]), ALU.is_equal).then_inc(onehot_ok, 1)
                if front.exists():
                    p = front.par
                    wait_quad(dve, xnT_full, front)
                    wait_quad(dve, gate_n_i, front + (-2))
                    dve.tensor_copy(xnT_hi[:, p, :], xnT[:, p, :]).then_inc(xnT_hi_ok, 1)
                if q.exists():
                    wait_quad(dve, conv2_done, q)
                    dve.scalar_tensor_tensor(out=work[:, T_, :], in0=bank[0][:], scalar=vec[:, V_T2:V_T2 + 1],
                                             in1=xnT[:, q.par, :], op0=ALU.add, op1=ALU.add).then_inc(xc_t, 1)
                    wait_quad(dve, xc_hi_ok, q)
                    dve.scalar_tensor_tensor(out=xc_lo[:, q.par, :], in0=work[:, T_, :], scalar=0.0,
                                             in1=f(xc_hi[:, q.par, :]), op0=ALU.max, op1=ALU.subtract
                                             ).then_inc(xc_lo_ok, 1)
                if front.exists():
                    wait_quad(dve, h1_full, front)
                    wait_quad(dve, conv2_done, front + (-2))
                    dve.tensor_copy(h1_hi[:, p, :, PAD:PAD + NODES],
                                    h1[:, p, :].rearrange("p (g t) -> p g t", g=QG)).then_inc(h1_hi_ok, 1)
                    wait_quad(dve, se_sq, front)
                    dve.tensor_copy(dist_l[0:3, p, :], dist_r[0:3, p, :]).then_inc(se_l, 1)
                if q.exists():
                    wait_quad(dve, tr_ok, q)
                    wait_quad(dve, gh_ok, q)
                    dve.scalar_tensor_tensor(out=work[:, W_, :], in0=work[:, TR, :], scalar=1.0,
                                             in1=work[:, GH, :], op0=ALU.add, op1=ALU.mult).then_inc(rgh_ok, 1)
                    wait_quad(dve, rgh_ok, q)
                    wait_quad(dve, gate_n_i, q)
                    dve.tensor_tensor(work[:, W_, :], bank[6][:], work[:, W_, :], ALU.add).then_inc(w_ok, 1)
                if back.exists():
                    wait_quad(dve, onehotT_done, back)
                    wait_quad(dve, w2_done[CHUNKS - 1], back + (-2))
                    dve.tensor_copy(onehotT[:, back.par, :], b1_bf[0:96, 0:TOK]).then_inc(onehotT_ok, 1)
                if q.exists():
                    wait_quad(dve, gru_d, q)
                    wait_quad(dve, tz_ok, q)
                    dve.scalar_tensor_tensor(out=work[:, DE, :], in0=work[:, TZ, :], scalar=1.0,
                                             in1=work[:, DE, :], op0=ALU.add, op1=ALU.mult).then_inc(gru_e, 1)
                    wait_quad(dve, gru_e, q)
                    wait_quad(dve, gruT_done, q + (-1))
                    dve.scalar_tensor_tensor(out=work[:, F_, :], in0=work[:, DE, :], scalar=0.5,
                                             in1=work[:, N_, :], op0=ALU.mult, op1=ALU.add).then_inc(gru_f, 1)

                def hidden(c):
                    wait_quad(dve, hid_hi_ok[c], back)
                    dve.scalar_tensor_tensor(out=hid_lo[:, c % 4, :], in0=bank[4 + HBANK[c % 4]][:], scalar=0.0,
                                             in1=f(hid_hi[:, c % 4, :]), op0=ALU.max, op1=ALU.subtract
                                             ).then_inc(hid_lo_ok[c], 1)

                if back.exists():
                    hidden(0)
                    hidden(1)
                if q.exists():
                    wait_quad(dve, gruT_done, q)
                    dve.tensor_tensor(x2[:, q.par, :, :], bank[3][:].rearrange("p (g d) -> p g d", g=QG),
                                      x_nat[:, q.par, :, :], ALU.add).then_inc(x2_ok, 1)
                if back.exists():
                    hidden(2)
                    hidden(3)
                if q.exists():
                    wait_quad(dve, x2_ok, q)
                    layer_stats(q, 2, x2, ln2_stats, ln2_mv, ln2_nv)
                if back.exists():
                    hidden(4)
                if front.exists():
                    wait_quad(dve, nmp_hi_ok, front)
                    dve.tensor_tensor(nmp_lo[:, front.par, :], bank[2][:], f(nmp_hi[:, front.par, :]),
                                      ALU.subtract).then_inc(nmp_lo_ok, 1)
                if back.exists():
                    for c in range(5, CHUNKS):
                        hidden(c)

            run_steps(dve, step)

        @block.tensor
        def _(pe):
            def raw(i):
                if i < TAPS:
                    return c2_raw.rearrange("p (i k) -> p i k", k=TAPS)[:, :, i]
                if i == W_CONV1:
                    return c1_raw
                if i < W_IH_NMP:
                    return ih_raw[:, (i - W_IH_CONV) * 256:(i - W_IH_CONV) * 256 + 128]
                if i < W_HH:
                    return ih_raw[:, (i - W_IH_NMP) * 256 + 128:(i - W_IH_NMP) * 256 + 256]
                if i < W_MSG:
                    return hh_raw[:, (i - W_HH) * 128:(i - W_HH) * 128 + 128]
                return msg_raw

            pe.wait_ge(pool_setup, 8)
            pe.wait_ge(w_loaded, 16 * 9)
            pe.wait_ge(bn_scaled, 1)
            for g in range(7):
                for k in range(4):
                    last = pe.transpose(bank[g][:, k * 128:k * 128 + 128], raw(4 * g + k), ident[:])
                last.then_inc(w_turned, 1)
            pe.transpose(bank[7][:, 0:EXPERTS], rout_raw, ident[0:EXPERTS, 0:EXPERTS])
            pe.transpose(bank[7][:, EXPERTS:EXPERTS + SE_ROWS], se_raw, ident[0:SE_ROWS, 0:SE_ROWS]
                         ).then_inc(w_turned, 1)
            pe.wait_ge(w_lo, 8)

            def split3(dst, lo_col, cols, hi, lo, start, stop, w=None):
                wh, wl = w if w else (wt_hi[:, lo_col:lo_col + cols], wt_lo[:, lo_col:lo_col + cols])
                pe.matmul(dst, wh, hi, start=start, stop=False)
                pe.matmul(dst, wh, lo, start=False, stop=False)
                return pe.matmul(dst, wl, hi, start=False, stop=stop)

            def block_of(i, dst, hi, lo, start, stop):
                return split3(dst, i * 128, 128, hi, lo, start, stop)

            def conv2(q, taps):
                for k in taps:
                    last = block_of(W_CONV2 + k, bank[0][:], h1_hi[:, q.par, :, k:k + NODES],
                                    h1_lo[:, q.par, :, k:k + NODES], k == 0, k == TAPS - 1)
                return last

            def step(q):
                front, back, last_ = q + 1, q + (-1), q + (-2)
                if q.exists():
                    wait_quad(pe, h1_hi_ok, q)
                    wait_quad(pe, h1_lo_ok, q)
                    wait_quad(pe, msg_ok, q)
                    conv2(q, range(0, 3))
                if last_.exists():
                    wait_quad(pe, o_ok, last_)
                    if back.exists():
                        wait_quad(pe, x2_ok, back)
                    for g in range(QG):
                        last = pe.transpose(bank[3][:, g * 128:g * 128 + 128],
                                            work[:, O_, g * 128:g * 128 + 128], ident[:])
                    last.then_inc(ffnT_done, 1)
                if back.exists():
                    wait_quad(pe, yn_ready, back)
                    wait_quad(pe, o_ok, back + (-1))
                    for g in range(QG):
                        last = pe.transpose(bank[1][:, g * 128:g * 128 + 128], yn[:, back.par, g, :], ident[:])
                    last.then_inc(ynT_done, 1)
                if q.exists():
                    conv2(q, range(3, 8))
                if back.exists():
                    wait_quad(pe, yn_hi_ok, back)
                    wait_quad(pe, yn_lo_ok, back)
                    if q.exists():
                        wait_quad(pe, nmp_lo_ok, q)
                    split3(bank[2][0:EXPERTS, :], ROUTER_COL, EXPERTS, yn_hi[:, back.par, :],
                           yn_lo[:, back.par, :], True, True).then_inc(router_done, 1)
                if q.exists():
                    conv2(q, range(8, 13))
                if back.exists():
                    pass_quad(pe, logitT_ok, back, pe_passed)
                    for g in range(QG):
                        last = pe.transpose(bank[1][:, g * EXPERTS:(g + 1) * EXPERTS],
                                            logitT[:, g * 128:g * 128 + 128], ident[0:EXPERTS, 0:EXPERTS])
                    last.then_inc(logit_done, 1)
                if q.exists():
                    conv2(q, range(13, TAPS)).then_inc(conv2_done, 1)
                if front.exists():
                    p = front.par
                    wait_quad(pe, xn_ready, front)
                    if q.exists():
                        wait_quad(pe, nmp_lo_ok, q)
                    if back.exists():
                        pass_quad(pe, logitT_ok, back, pe_passed)
                    for g in range(QG):
                        last = pe.transpose(bank[2][:, g * 128:g * 128 + 128], xn[:, p, g, :], ident[:])
                    last.then_inc(xnT_done, 1)
                    wait_dma(pe, adj_loaded, front)
                    if last_.exists():
                        wait_quad(pe, y_ok, last_)
                    elif back.exists():
                        wait_quad(pe, x2_ok, back)
                    for g in range(QG):
                        last = pe.transpose(bank[3][:, g * 128:g * 128 + 128], adj_nat[:, p, g, :], ident[:])
                    last.then_inc(adjT_done, 1)
                if q.exists():
                    s = q.par
                    if last_.exists():
                        for c in range(4, CHUNKS):
                            wait_quad(pe, hid_lo_ok[c], last_)
                    if back.exists() and not last_.exists():
                        wait_quad(pe, w_ok, back)
                    xh, xl, nh, nl = xnT_hi[:, s, :], xnT_lo[:, s, :], nmp_hi[:, s, :], nmp_lo[:, s, :]
                    block_of(W_HH + 2, bank[7][:], xh, xl, True, True).then_inc(gate_n_h, 1)
                    wait_quad(pe, nmp_hi_ok, q)
                    wait_quad(pe, nmp_lo_ok, q)
                    for i in range(2):
                        block_of(W_HH + i, bank[4 + i][:], xh, xl, True, False)
                        block_of(W_IH_NMP + i, bank[4 + i][:], nh, nl, False, False)
                    block_of(W_IH_NMP + 2, bank[6][:], nh, nl, True, False)
                if front.exists():
                    wait_quad(pe, xnT_hi_ok, front)
                    wait_quad(pe, xnT_lo_ok, front)
                    block_of(W_CONV1, bank[2][:], xnT_hi[:, p, :], xnT_lo[:, p, :], True, True
                             ).then_inc(conv1_done, 1)
                    wait_quad(pe, adjT_ok, front)
                    split3(bank[3][0:SE_ROWS, :], SE_COL, SE_ROWS, xnT_hi[:, p, :], xnT_lo[:, p, :], True, True
                           ).then_inc(se_done, 1)
                if q.exists():
                    wait_quad(pe, xc_hi_ok, q)
                    wait_quad(pe, xc_lo_ok, q)
                    for i, done in enumerate((gate_r, gate_z, gate_n_i)):
                        block_of(W_IH_CONV + i, bank[4 + i][:], xc_hi[:, s, :], xc_lo[:, s, :], False, True
                                 ).then_inc(done, 1)
                if front.exists():
                    if q.exists():
                        wait_quad(pe, xc_t, q)
                    for g in range(QG):
                        pe.matmul(bank[0][:, g * 128:g * 128 + 128], ones_bf[:], bmsg_parts[:],
                                  start=True, stop=False)
                        last = pe.matmul(bank[0][:, g * 128:g * 128 + 128], xnT[:, p, g * 128:g * 128 + 128],
                                         wmsg[:], start=False, stop=True)
                    last.then_inc(msg_done, 1)
                if back.exists():
                    wait_quad(pe, onehot_ok, back)
                    for g in range(QG):
                        last = pe.transpose(b1_bf[0:96, g * 128:g * 128 + 128],
                                            onehot[:, g, :, :].rearrange("p r e -> p (r e)"), ident_bf[:])
                    last.then_inc(onehotT_done, 1)
                if front.exists():
                    wait_quad(pe, h1_full, front)
                    wait_quad(pe, se_sq, front)
                    wait_quad(pe, se_l, front)
                    for g in range(QG):
                        cols = slice(g * 128, g * 128 + 128)
                        last = pe.matmul(bank[2][:, cols], dist_l[:, p, cols], dist_r[:, p, cols],
                                         start=True, stop=True)
                    last.then_inc(dist_done, 1)

                def hidden(c):
                    dst = bank[4 + HBANK[c % 4]][:]
                    if c >= 4:
                        wait_quad(pe, hid_lo_ok[c - 4], back)
                    elif q.exists():
                        wait_quad(pe, (tr_ok, tz_ok, gh_ok, w_ok)[c], q)
                    else:
                        wait_quad(pe, hid_lo_ok[c + 4], back + (-1))
                    cols = slice(c * 128, c * 128 + 128)
                    split3(dst, 0, 0, yn_hi[:, back.par, :], yn_lo[:, back.par, :], True, False,
                           (w1_hi[:, cols], w1_lo[:, cols]))
                    pe.matmul(dst, b1_or_off[:, cols], onehotT[:, back.par, :], start=False, stop=True
                              ).then_inc(w1_done[c], 1)

                def project(c):
                    wait_quad(pe, hid_hi_ok[c], back)
                    wait_quad(pe, hid_lo_ok[c], back)
                    split3(bank[1][:], 0, 0, hid_hi[:, c % 4, :], hid_lo[:, c % 4, :], False, c == CHUNKS - 1,
                           (w2_hi[:, c, :], w2_lo[:, c, :])).then_inc(w2_done[c], 1)

                if back.exists():
                    wait_quad(pe, onehotT_ok, back)
                    if back.n == 0 and back.it is None:
                        pe.wait_ge(consts, 1)
                        pe.wait_ge(f_split, 2)
                    pe.matmul(bank[1][:], b2_parts[:], onehotT[:, back.par, :], start=True, stop=False)
                    for c in range(3):
                        hidden(c)
                    project(0)
                if q.exists():
                    wait_quad(pe, gru_f, q)
                    if front.exists():
                        wait_quad(pe, se_sq, front)
                    elif last_.exists():
                        wait_quad(pe, y_ok, last_)
                    for g in range(QG):
                        last = pe.transpose(bank[3][:, g * 128:g * 128 + 128],
                                            work[:, F_, g * 128:g * 128 + 128], ident[:])
                    last.then_inc(gruT_done, 1)
                if back.exists():
                    for c in range(3, 6):
                        hidden(c)
                        project(c - 2)
                if front.exists():
                    wait_quad(pe, exp_ok, front)
                    wait_quad(pe, att_ok, front)
                    wait_quad(pe, msg_ok, front)
                    for g in range(QG):
                        cols = slice(g * 128, g * 128 + 128)
                        last = pe.matmul(bank[2][:, cols], msg[:, p, cols], att[:, p, cols], start=True, stop=True)
                    last.then_inc(nmp_done, 1)
                if back.exists():
                    for c in range(6, CHUNKS):
                        hidden(c)
                        project(c - 2)
                    project(CHUNKS - 2)
                    project(CHUNKS - 1)

            run_steps(pe, step)


def kernel(**inputs):
    import concourse.bacc as bacc
    from concourse.bass_utils import run_bass_kernel_spmd

    nc = bacc.Bacc("TRN2", target_bir_lowering=False, num_devices=1)
    arrays, args = {}, {}
    for name, value in inputs.items():
        value = np.ascontiguousarray(value)
        arrays[f"in_{name}"] = value
        args[name] = nc.dram_tensor(f"in_{name}", value.shape, mybir.dt.from_np(value.dtype),
                                    kind="ExternalInput").ap()
    out = nc.dram_tensor("out", (GRAPHS, NODES, D), mybir.dt.float32, kind="ExternalOutput").ap()
    program(nc, args, out)
    result = run_bass_kernel_spmd(nc, [arrays], core_ids=[0])
    return np.asarray(result.results[0]["out"])
```

```python
from contextlib import ExitStack

import numpy as np
import concourse.bass as bass
from concourse import mybir

GRAPHS, NODES, D = 128, 128, 128
TAPS = 17
PAD = TAPS // 2
EXPERTS, HID = 32, 32
EPS = 1e-5
QG = 4
QUADS = GRAPHS // QG
TOK = QG * NODES
PADDED = NODES + 2 * PAD
TOKENS = GRAPHS * NODES
TILE = 128
TILES = (TOKENS + EXPERTS * (TILE - 1)) // TILE
TILES += -TILES % 8
FILLS = 16
R_X, R_N, R_ID, ROW = 0, D, 2 * D, 2 * D + 4
NO_TOKEN = 1 << 20
TG = 4
GROUPS = TILES // TG
LOOP_FIRST, LOOP_LAST = 4, 29
BN_VECTORS, VECTORS = 8, 14
W_CONV2, W_CONV1 = 0, TAPS
W_IH_CONV = TAPS + 1
W_IH_NMP = W_IH_CONV + 3
W_HH = W_IH_NMP + 3
W_MSG = W_HH + 3
W_SMALL = W_MSG + 1
ROUTER_COL = W_SMALL * 128
SE_COL = ROUTER_COL + EXPERTS
SE_ROWS = 67
WT_COLS = SE_COL + SE_ROWS


class Step:

    def __init__(self, n, it=None):
        self.n, self.it, self.par, self.lap = n, it, n % 2, n % self.every

    def __add__(self, k):
        return type(self)(self.n + k, self.it)

    def exists(self):
        return self.it is not None or 0 <= self.n < self.count

    def index(self):
        return self.n if self.it is None else self.every * self.it + self.n

    def events(self):
        return self.n + 1 if self.it is None else self.every * self.it + (self.n + 1)

    def loads(self):
        n = self.n // self.every + 1
        return 16 * n if self.it is None else 16 * self.it + 16 * n


class Quad(Step):
    count, every = QUADS, 2


class Group(Step):
    count, every = GROUPS, 4


def wait_quad(eng, sem, q):
    if q.n >= 0:
        eng.wait_ge(sem, q.events())


def pass_quad(eng, sem, q, passed):
    if q.n >= 0:
        eng.wait_ge(sem, q.events())
        eng.sem_inc(passed, 1)


def wait_dma(eng, sems, q):
    if q.n >= 0:
        eng.wait_ge(sems[q.lap], q.loads())


def run_steps(eng, step):
    for n in range(-1, LOOP_FIRST):
        step(Quad(n))
    with eng.Fori(0, (LOOP_LAST - LOOP_FIRST + 1) // 2) as it:
        for k in range(2):
            step(Quad(LOOP_FIRST + k, it))
    for n in range(LOOP_LAST + 1, QUADS + 2):
        step(Quad(n))


def run_groups(eng, step):
    for n in range(4):
        step(Group(n))
    with eng.Fori(0, GROUPS // 4 - 1) as it:
        for k in range(4):
            step(Group(4 + k, it))
    for n in range(GROUPS, GROUPS + 2):
        step(Group(n))


def program(nc, a, out):
    f32, f32r, bf16 = mybir.dt.float32, mybir.dt.float32r, mybir.dt.bfloat16
    i32, u32 = mybir.dt.int32, mybir.dt.uint32
    ALU, ACT, AX = mybir.AluOpType, mybir.ActivationFunctionType, mybir.AxisListType
    ctx = ExitStack()

    def sb(name, shape, dt=f32):
        return ctx.enter_context(nc.sbuf_tensor(name, shape, dt))

    def sem(name):
        return ctx.enter_context(nc.semaphore(name))

    def sems(name, n):
        return [sem(f"{name}{i}") for i in range(n)]

    with ctx:
        x_v = a["x"].rearrange("(q g) t d -> q t g d", g=QG)
        adj_v = a["adj"].rearrange("(q g) t d -> q t g d", g=QG)
        out_rows = out.rearrange("b t d -> (b t) d")
        sorted_rows = nc.dram_tensor("sorted_rows", [TILES * TILE, ROW], f32).ap()
        groups_v = sorted_rows.rearrange("(n t p) c -> n p t c", t=TG, p=TILE)

        wt_hi = sb("wt_hi", [128, WT_COLS], f32r)
        wt_lo = sb("wt_lo", [128, WT_COLS], f32r)
        wmsg = sb("wmsg", [128, 128])
        w1b1 = sb("w1b1", [128, EXPERTS, HID + 1])
        b1_nat, b1_turned = sb("b1_nat", [EXPERTS, HID]), sb("b1_turned", [HID, EXPERTS])
        w2b2 = sb("w2b2", [HID + 1, EXPERTS * D])
        bmsg_parts = sb("bmsg_parts", [65, 128], bf16)
        ones_bf = sb("ones_bf", [128, 128], bf16)
        earlier = sb("earlier", [128, 128], bf16)
        ident = sb("ident", [128, 128])
        rank = sb("rank", [128, EXPERTS])
        expert_no = sb("expert_no", [128, EXPERTS])
        minus_half = sb("minus_half", [128, QG])
        (V_G1, V_B1, V_M1, V_V1, V_G2, V_B2, V_M2, V_V2, V_IHR, V_IHZ, V_IHN, V_HHR, V_HHZ, V_HHN,
         V_S1, V_S2, V_T1, V_T2, V_HR, V_HZ, V_HN) = range(21)
        vec = sb("vec", [128, 21])
        bse = sb("bse", [SE_ROWS, 1])
        brout = sb("brout", [EXPERTS, 1])

        x_nat = sb("x_nat", [128, 2, QG, D])
        x_keep = sb("x_keep", [128, 2, QG, D])
        adj_nat = sb("adj_nat", [128, 2, QG, NODES])
        xn = sb("xn", [128, 2, QG, D])
        xnT = sb("xnT", [128, 2, TOK])
        xnT_hi = sb("xnT_hi", [128, 2, TOK], f32r)
        xnT_lo = sb("xnT_lo", [128, 2, TOK], f32r)
        adjT = sb("adjT", [128, 2, TOK])
        h1 = sb("h1", [128, 2, TOK])
        h1_hi = sb("h1_hi", [128, 2, QG, PADDED], f32r)
        h1_lo = sb("h1_lo", [128, 2, QG, PADDED], f32r)
        dist_l = sb("dist_l", [SE_ROWS, 2, TOK])
        dist_r = sb("dist_r", [SE_ROWS, 2, TOK])
        msg = sb("msg", [128, 2, TOK])
        att = sb("att", [128, 2, TOK])
        nmp_hi = sb("nmp_hi", [128, 2, TOK], f32r)
        nmp_lo = sb("nmp_lo", [128, 2, TOK], f32r)
        xc_hi = sb("xc_hi", [128, 2, TOK], f32r)
        xc_lo = sb("xc_lo", [128, 2, TOK], f32r)
        row = sb("row", [128, 4, QG, ROW])
        yn_hi = sb("yn_hi", [128, TOK], f32r)
        yn_lo = sb("yn_lo", [128, TOK], f32r)
        work = sb("work", [128, 9, TOK])
        (E_, T_, GH, TR, TZ, W_, N_, DE, F_) = range(9)
        logitT = sb("logitT", [EXPERTS, TOK])
        lmax = sb("lmax", [128, QG])
        ranked = sb("ranked", [128, QG, EXPERTS])
        first = sb("first", [128, QG])
        onehot = sb("onehot", [128, QG, EXPERTS], bf16)
        stats = sb("stats", [128, 2, QG, 6])
        mv = sb("mv", [128, 2, QG, 2])
        negm = sb("negm", [128, 4, QG])
        veps = sb("veps", [128, 4, QG])
        rstd = sb("rstd", [128, 4, QG])

        free = sb("free", [128, EXPERTS])
        end = sb("end", [128, EXPERTS])
        opened = sb("opened", [128, 1])
        ranked_counts = sb("ranked_counts", [128, (QG + 1) * EXPERTS])
        bounds = sb("bounds", [128, TOK // TILE])
        past = sb("past", [128, TOK // TILE, EXPERTS])
        over = sb("over", [128, EXPERTS])
        opens = sb("opens", [128, EXPERTS])
        news = sb("news", [128, EXPERTS])
        SHIFT = EXPERTS // 2
        run = sb("run", [128, 2, SHIFT + EXPERTS])
        new_end = sb("new_end", [128, EXPERTS])
        new_base = sb("new_base", [128, EXPERTS])
        off_new = sb("off_new", [128, EXPERTS])
        off_open = sb("off_open", [128, EXPERTS])
        slot_e = sb("slot_e", [128, QG, EXPERTS])
        in_open = sb("in_open", [128, QG, EXPERTS])
        slot_f = sb("slot_f", [128, QG])
        slot = sb("slot", [128, 2, QG], i32)
        token = sb("token", [128, QG])
        HALVES = -(-TILES // 128)
        tile_start = sb("tile_start", [128, HALVES])
        has_tile = sb("has_tile", [128, HALVES, EXPERTS])
        tile_cmp = sb("tile_cmp", [128, HALVES, EXPERTS])
        tile_e = sb("tile_e", [128, HALVES])
        tile_expert = sb("tile_expert", [1, HALVES * 128], i32)

        rows_in = row
        ids = sb("ids", [128, 4, TG], i32)
        t_ynT = xnT
        t_w1 = sb("t_w1", [128, 2, TG, HID + 1])
        t_hid = sb("t_hid", [HID + 1, 2, TOK])
        t_out = xn

        flat = work[:, :, :].rearrange("p a n -> p (a n)")
        c2_raw = flat[:, 0:2176]
        ih_raw = flat[:, 2176:2944]
        hh_raw = flat[:, 2944:3328]
        c1_raw = flat[:, 3328:3456]
        msg_raw = flat[:, 3456:3584]
        rout_raw = flat[0:EXPERTS, 3584:3712]
        se_raw = flat[0:SE_ROWS, 3712:3840]
        bm_raw = flat[0:65, 3840:3968]
        bm_rest = flat[0:65, 3968:4096]
        fill_row = sb("fill_row", [128, ROW])[:, :]
        bm_p = sb("bm_p", [65, 128], bf16)
        ints = sb("ints", [128, EXPERTS], i32)

        bank = [ctx.enter_context(nc.psum_tensor(f"bank{i}", [128, TOK], f32)) for i in range(8)]

        x_loaded, adj_loaded, scattered = sems("x_loaded", 2), sems("adj_loaded", 2), sems("scattered", 2)
        w_loaded, bn_loaded, v_loaded, e_loaded, filled = (sem(n) for n in (
            "w_loaded", "bn_loaded", "v_loaded", "e_loaded", "filled"))
        pool_setup, bn_pow, bn_vec, bn_scaled, dve_setup, state_zero, bmsg_ok = (sem(n) for n in (
            "pool_setup", "bn_pow", "bn_vec", "bn_scaled", "dve_setup", "state_zero", "bmsg_ok"))
        zeroed, template, w_turned, w_hi, w_lo = (sem(n) for n in (
            "zeroed", "template", "w_turned", "w_hi_done", "w_lo_done"))
        (ln1_stats, ln1_mv, ln1_nv, ln1_rstd, xn_ready, x_kept, xnT_done, xnT_full, xnT_hi_ok, xnT_lo_ok,
         adjT_done, adjT_ok, conv1_done, h1_full, h1_hi_ok, h1_lo_ok, se_done, se_sq, se_l, msg_done,
         msg_ok, dist_done, exp_ok, att_ok, nmp_done, nmp_hi_ok, nmp_lo_ok, conv2_done, xc_t, xc_hi_ok,
         xc_lo_ok, gate_n_h, gate_r, gate_z, gate_n_i, gh_ok, tr_ok, tz_ok, rgh_ok, w_ok, n_ok, gru_d,
         gru_e, gru_f, gruT_done, x2_ok, ln2_stats, ln2_mv, ln2_nv, ln2_rstd, yn_ready, ynT_done,
         yn_hi_ok, yn_lo_ok, router_done, logitT_ok, logit_done, am_max, am_eq, am_rank, am_first,
         onehot_ok, counted, ranks_kept, slots_ok) = (
            sem(n) for n in """ln1_stats ln1_mv ln1_nv ln1_rstd xn_ready x_kept xnT_done xnT_full
            xnT_hi_ok xnT_lo_ok adjT_done adjT_ok conv1_done h1_full h1_hi_ok h1_lo_ok se_done se_sq
            se_l msg_done msg_ok dist_done exp_ok att_ok nmp_done nmp_hi_ok nmp_lo_ok conv2_done xc_t
            xc_hi_ok xc_lo_ok gate_n_h gate_r gate_z gate_n_i gh_ok tr_ok tz_ok rgh_ok w_ok n_ok gru_d
            gru_e gru_f gruT_done x2_ok ln2_stats ln2_mv ln2_nv ln2_rstd yn_ready ynT_done yn_hi_ok
            yn_lo_ok router_done logitT_ok logit_done am_max am_eq am_rank am_first onehot_ok
            counted ranks_kept slots_ok""".split())
        ROUTE_STEPS = 16
        route = sems("route", ROUTE_STEPS)
        table_sum, table_row, table_ok = sem("table_sum"), sem("table_row"), sem("table_ok")
        rows_loaded, t_scattered = sems("rows_loaded", 4), sems("t_scattered", 4)
        (t_turned, t_ynT_ok, t_w1_ok, t_hid_done, t_hid_ok, t_out_done, t_out_ok) = (
            sem(n) for n in "t_turned t_ynT_ok t_w1_ok t_hid_done t_hid_ok t_out_done t_out_ok".split())
        dve_passed, pool_passed, pe_passed = sem("dve_passed"), sem("pool_passed"), sem("pe_passed")

        def f(ap):
            return ap.bitcast(f32)

        def by_graph(ap):
            return ap.rearrange("p (g n) -> p g n", g=QG)

        def over_graphs(ap):
            return ap.rearrange("p (o e) -> p o e", o=1).to_broadcast([128, QG, EXPERTS])

        def wait_scatter(eng, q):
            if q.n >= 0:
                eng.wait_ge(scattered[q.par], QG * q.loads())

        def wait_tiles_scattered(eng, n):
            if n.n >= 0:
                eng.wait_ge(t_scattered[n.lap], TG * n.loads())

        block = ctx.enter_context(nc.Block())

        @block.sync
        def _(sp):
            def load_x(q):
                sp.dma_start(x_nat[:, q.par, :, :], x_v[bass.ds(q.index(), 1)][0]).then_inc(x_loaded[q.par], 16)

            def load_adj(q):
                sp.dma_start(adj_nat[:, q.par, :, :], adj_v[bass.ds(q.index(), 1)][0]
                             ).then_inc(adj_loaded[q.par], 16)

            load_x(Quad(0))
            sp.dma_start(c2_raw, a["L0_gnn_conv2_w"].rearrange("o i k -> o (i k)")).then_inc(w_loaded, 16)
            sp.dma_start(c1_raw, a["L0_gnn_conv1_w"].rearrange("o i k -> o (i k)")).then_inc(w_loaded, 16)
            sp.dma_start(ih_raw.rearrange("p (g c) -> p g c", g=3),
                         a["L0_gnn_w_ih"].rearrange("(g o) c -> o g c", g=3)).then_inc(w_loaded, 16)
            sp.dma_start(hh_raw.rearrange("p (g c) -> p g c", g=3),
                         a["L0_gnn_w_hh"].rearrange("(g o) c -> o g c", g=3)).then_inc(w_loaded, 16)
            sp.dma_start(msg_raw, a["L0_gnn_w_msg"]).then_inc(w_loaded, 16)
            sp.dma_start(rout_raw, a["L0_ffn_router_w"]).then_inc(w_loaded, 16)
            sp.wait_ge(zeroed, 1)
            for r in (0, 32, 64):
                sp.dma_start(se_raw[r:r + 3, :], a["L0_gnn_w_se"]).then_inc(w_loaded, 16)

            def step(q):
                ahead, front = q + 2, q + 1
                if front.exists():
                    wait_quad(sp, adjT_done, front + (-2))
                    load_adj(front)
                if ahead.exists():
                    wait_quad(sp, x_kept, ahead + (-2))
                    wait_quad(sp, xn_ready, ahead + (-2))
                    load_x(ahead)

            run_steps(sp, step)

            for p in range(2):
                sp.wait_ge(scattered[p], 16 * QG * QUADS // 2)
            sp.wait_ge(filled, 16 * FILLS)

            def step(n):
                if n.exists():
                    wait_quad(sp, t_out_ok, n + (-4))
                    sp.dma_start(rows_in[:, n.lap, :, :], groups_v[bass.ds(n.index(), 1)][0]
                                 ).then_inc(rows_loaded[n.lap], 16)

            run_groups(sp, step)

        @block.gpsimd
        def _(pool):
            done_ops = [0]

            def link(ins):
                done_ops[0] += 1
                ins.then_inc(pool_setup, 1)
                pool.wait_ge(pool_setup, done_ops[0])

            link(pool.memset(se_raw, 0.0))
            link(pool.memset(bm_raw, 0.0))
            link(pool.memset(w1b1[:].rearrange("p e h -> p (e h)"), 0.0))
            pool.sem_inc(zeroed, 1)
            link(pool.memset(ident[:], 0.0))
            link(pool.affine_select(out=ident[:], in_=ident[:], compare_op=ALU.not_equal, fill=1.0, base=0,
                                    pattern=[[-1, 128]], channel_multiplier=1))
            link(pool.memset(minus_half[:], -0.5))
            link(pool.memset(ones_bf[:], 1.0))
            pool.wait_ge(bn_vec, 1)
            link(pool.tensor_tensor(vec[:, V_V1:V_V1 + 1], vec[:, V_V1:V_V1 + 1], minus_half[:, 0:1], ALU.pow))
            pool.tensor_tensor(vec[:, V_V2:V_V2 + 1], vec[:, V_V2:V_V2 + 1], minus_half[:, 0:1], ALU.pow
                               ).then_inc(bn_pow, 1)
            pool.wait_ge(bn_pow, 1)
            link(pool.memset(f(h1_hi[:]).rearrange("p a g n -> p (a g n)"), 0.0))
            link(pool.memset(f(h1_lo[:]).rearrange("p a g n -> p (a g n)"), 0.0))
            link(pool.memset(dist_l[:], 0.0))
            link(pool.memset(dist_r[:], 0.0))
            link(pool.memset(dist_l[32:35, :, :], -0.5))
            link(pool.memset(dist_r[64:67, :, :], -0.5))
            link(pool.affine_select(out=earlier[:], in_=ones_bf[:], compare_op=ALU.is_gt, fill=0.0, base=0,
                                    pattern=[[1, 128]], channel_multiplier=-1))
            for dst, pattern, base, per_row in ((rank[:], [[-1, EXPERTS]], EXPERTS, 0),
                                                (expert_no[:], [[1, EXPERTS]], 0, 0),
                                                (bounds[:], [[TILE, TOK // TILE]], 0, 0),
                                                (token[:], [[NODES, QG]], -TOK, 1),
                                                (tile_start[:], [[128 * TILE, HALVES]], 0, TILE)):
                part = ints[:, 0:dst.shape[1]]
                link(pool.iota(part, pattern=pattern, base=base, channel_multiplier=per_row))
                link(pool.tensor_copy(dst, part))
            for state in (free, end, opened, has_tile, run):
                link(pool.memset(state[:], 0.0))
            link(pool.memset(row[:, 0:2, :, R_ID:ROW], 0.0))
            link(pool.memset(t_hid[HID:HID + 1, :, :], 1.0))
            pool.sem_inc(state_zero, 1)

            def rstd_and_normalize(q, k, nv, rstd_ok, src, dst, done):
                p = q.par
                wait_quad(pool, nv, q)
                pool.tensor_tensor(rstd[:, k + p, :], veps[:, k + p, :], minus_half[:], ALU.pow
                                   ).then_inc(rstd_ok, 1)
                pass_quad(pool, rstd_ok, q, pool_passed)
                for g in range(QG):
                    last = pool.tensor_scalar(dst[:, p, g, :], src[:, p, g, :], negm[:, k + p, g:g + 1],
                                              rstd[:, k + p, g:g + 1], ALU.add, ALU.mult)
                last.then_inc(done, 1)

            def step(q):
                front, back, old = q + 1, q + (-1), q + (-2)
                if front.exists():
                    p = front.par
                    wait_quad(pool, xnT_done, front + (-2))
                    rstd_and_normalize(front, 0, ln1_nv, ln1_rstd, x_nat, xn, xn_ready)
                if back.exists():
                    rstd_and_normalize(back, 2, ln2_nv, ln2_rstd, row[:, :, :, R_X:R_X + D],
                                       row[:, :, :, R_N:R_N + D], yn_ready)
                if front.exists():
                    wait_quad(pool, xnT_hi_ok, front)
                    pool.tensor_tensor(xnT_lo[:, p, :], xnT[:, p, :], f(xnT_hi[:, p, :]), ALU.subtract
                                       ).then_inc(xnT_lo_ok, 1)
                if old.exists():
                    if old.n == 0 and old.it is None:
                        pool.wait_ge(filled, 16 * FILLS)
                    pass_quad(pool, slots_ok, old, pool_passed)
                    for g in range(QG):
                        pool.indirect_dma_start(
                            out=sorted_rows[:, :],
                            out_offset=bass.IndirectOffsetOnAxis(ap=slot[:, old.par, g:g + 1].bitcast(u32), axis=0),
                            in_=row[:, old.par, g, :], in_offset=None, bounds_check=TILES * TILE - 1,
                            oob_is_err=False).then_inc(scattered[old.par], 16)
                if front.exists():
                    wait_quad(pool, h1_hi_ok, front)
                    pool.tensor_tensor(h1_lo[:, p, :, PAD:PAD + NODES], by_graph(h1[:, p, :]),
                                       f(h1_hi[:, p, :, PAD:PAD + NODES]), ALU.subtract).then_inc(h1_lo_ok, 1)
                if q.exists():
                    wait_quad(pool, n_ok, q)
                    pool.tensor_tensor(work[:, DE, :], xnT[:, q.par, :], work[:, N_, :], ALU.subtract
                                       ).then_inc(gru_d, 1)
                if front.exists():
                    wait_quad(pool, exp_ok, front)
                    wait_quad(pool, adjT_ok, front)
                    wait_quad(pool, nmp_done, front + (-2))
                    pool.tensor_tensor(att[:, p, :], work[:, E_, :], adjT[:, p, :], ALU.mult
                                       ).then_inc(att_ok, 1)

            run_steps(pool, step)

            def step(n):
                done = n + (-2)
                if done.exists():
                    pass_quad(pool, t_out_ok, done, pool_passed)
                    for t in range(TG):
                        pool.indirect_dma_start(
                            out=out_rows[:, :],
                            out_offset=bass.IndirectOffsetOnAxis(
                                ap=ids[:, done.lap, t:t + 1].bitcast(u32), axis=0),
                            in_=t_out[:, done.par, t, :], in_offset=None, bounds_check=TOKENS - 1,
                            oob_is_err=False).then_inc(t_scattered[done.lap], 16)

            run_groups(pool, step)
            for lap in range(4):
                pool.wait_ge(t_scattered[lap], 16 * TG * GROUPS // 4)

        @block.scalar
        def _(act):
            for col, name in ((V_V1, "bn1_v"), (V_V2, "bn2_v"), (V_G1, "bn1_g"), (V_G2, "bn2_g"),
                              (V_B1, "bn1_b"), (V_M1, "bn1_m"), (V_B2, "bn2_b"), (V_M2, "bn2_m")):
                act.dma_start(vec[:, col:col + 1], a["L0_gnn_" + name].rearrange("(p o) -> p o", o=1)
                              ).then_inc(bn_loaded, 16)
            for col, name in ((V_IHR, "b_ih"), (V_HHR, "b_hh")):
                for g in range(3):
                    act.dma_start(vec[:, col + g:col + g + 1],
                                  a["L0_gnn_" + name][g * 128:g * 128 + 128].rearrange("(p o) -> p o", o=1)
                                  ).then_inc(v_loaded, 16)
            for r in (0, 32, 64):
                act.dma_start(bse[r:r + 3, :], a["L0_gnn_b_se"].rearrange("(p o) -> p o", o=1)
                              ).then_inc(v_loaded, 16)
            act.dma_start(brout[:], a["L0_ffn_router_b"].rearrange("(p o) -> p o", o=1)).then_inc(v_loaded, 16)
            act.dma_start(b1_nat[:], a["L0_ffn_b1"]).then_inc(v_loaded, 16)
            act.wait_ge(zeroed, 1)
            for r in (0, 32, 64):
                act.dma_start(bm_raw[r:r + 1, :], a["L0_gnn_b_msg"].rearrange("(o p) -> o p", o=1)
                              ).then_inc(v_loaded, 16)
            for g in range(8):
                act.wait_ge(w_turned, g + 1)
                lo, hi = g * 512, min(g * 512 + 512, WT_COLS)
                if g == W_MSG // 4:
                    k = (W_MSG % 4) * 128
                    act.activation(wmsg[:], bank[g][:, k:k + 128], ACT.Copy)
                act.activation(wt_hi[:, lo:hi], bank[g][:, 0:hi - lo], ACT.Copy).then_inc(w_hi, 1)
            act.wait_ge(v_loaded, 16 * VECTORS)
            act.wait_ge(bn_vec, 2)
            act.wait_ge(template, 1)

            def fill(parts):
                per = TILES // FILLS
                for n in parts:
                    act.dma_start(sorted_rows[n * per * TILE:(n + 1) * per * TILE, :]
                                  .rearrange("(t p) c -> p t c", p=TILE),
                                  fill_row.rearrange("p (o c) -> p o c", o=1).to_broadcast([128, per, ROW])
                                  ).then_inc(filled, 16)

            def step(q):
                front, back = q + 1, q + (-1)
                if q.it is None and 0 <= q.n < 2:
                    fill(range(q.n * FILLS // 2, (q.n + 1) * FILLS // 2))
                if q.it is None and q.n == 2:
                    act.dma_start(w1b1[:, :, 0:HID], a["L0_ffn_W1"].rearrange("e d h -> d e h")).then_inc(e_loaded, 16)
                    act.dma_start(w2b2[0:HID, :].rearrange("p (e d) -> p e d", e=EXPERTS),
                                  a["L0_ffn_W2"].rearrange("e h d -> h e d")).then_inc(e_loaded, 16)
                    act.dma_start(w2b2[HID:HID + 1, :], a["L0_ffn_b2"].rearrange("(o e) d -> o (e d)", o=1)
                                  ).then_inc(e_loaded, 16)
                if q.exists():
                    wait_quad(act, nmp_done, q)
                    wait_quad(act, gate_n_i, q + (-2))
                    act.activation(nmp_hi[:, q.par, :], bank[2][:], ACT.Copy).then_inc(nmp_hi_ok, 1)
                if front.exists():
                    p = front.par
                    wait_dma(act, x_loaded, front)
                    wait_quad(act, x2_ok, front + (-2))
                    act.activation(x_keep[:, p, :, :], x_nat[:, p, :, :], ACT.Copy).then_inc(x_kept, 1)
                    wait_quad(act, xnT_done, front)
                    wait_quad(act, gru_d, front + (-2))
                    act.activation(xnT[:, p, :], bank[2][:], ACT.Copy).then_inc(xnT_full, 1)
                    wait_quad(act, adjT_done, front)
                    wait_quad(act, att_ok, front + (-2))
                    act.activation(adjT[:, p, :], bank[3][:], ACT.Copy).then_inc(adjT_ok, 1)
                if q.exists():
                    wait_quad(act, xc_t, q)
                    wait_quad(act, gate_n_i, q + (-2))
                    act.activation(xc_hi[:, q.par, :], work[:, T_, :], ACT.Relu).then_inc(xc_hi_ok, 1)
                if back.exists():
                    wait_quad(act, ynT_done, back)
                    wait_quad(act, router_done, back + (-1))
                    act.activation(yn_hi[:], bank[1][:], ACT.Copy).then_inc(yn_hi_ok, 1)
                if q.exists():
                    wait_quad(act, gate_n_h, q)
                    wait_quad(act, rgh_ok, q + (-1))
                    act.activation(work[:, GH, :], bank[7][:], ACT.Identity, bias=vec[:, V_HN:V_HN + 1],
                                   scale=0.5).then_inc(gh_ok, 1)
                if front.exists():
                    wait_quad(act, conv1_done, front)
                    wait_quad(act, h1_lo_ok, front + (-2))
                    act.activation(h1[:, p, :], bank[2][:], ACT.Relu, bias=vec[:, V_T1:V_T1 + 1]
                                   ).then_inc(h1_full, 1)
                    wait_quad(act, se_done, front)
                    wait_quad(act, dist_done, front + (-2))
                    act.activation(dist_r[0:3, p, :], bank[3][0:3, :], ACT.Identity, bias=bse[0:3, :])
                    act.activation(dist_r[32:35, p, :], bank[3][32:35, :], ACT.Square, bias=bse[32:35, :])
                    act.activation(dist_l[64:67, p, :], bank[3][64:67, :], ACT.Square, bias=bse[64:67, :]
                                   ).then_inc(se_sq, 1)
                if back.exists():
                    wait_quad(act, router_done, back)
                    wait_quad(act, logit_done, back + (-1))
                    act.activation(logitT[:], bank[1][0:EXPERTS, :], ACT.Identity, bias=brout[:]
                                   ).then_inc(logitT_ok, 1)
                if q.exists():
                    wait_quad(act, gate_r, q)
                    act.activation(work[:, TR, :], bank[4][:], ACT.Tanh, bias=vec[:, V_HR:V_HR + 1],
                                   scale=0.5).then_inc(tr_ok, 1)
                    wait_quad(act, gate_z, q)
                    wait_quad(act, gru_e, q + (-1))
                    act.activation(work[:, TZ, :], bank[5][:], ACT.Tanh, bias=vec[:, V_HZ:V_HZ + 1],
                                   scale=0.5).then_inc(tz_ok, 1)
                    wait_quad(act, w_ok, q)
                    wait_quad(act, gru_f, q + (-1))
                    act.activation(work[:, N_, :], work[:, W_, :], ACT.Tanh, bias=vec[:, V_IHN:V_IHN + 1]
                                   ).then_inc(n_ok, 1)
                if front.exists():
                    wait_quad(act, dist_done, front)
                    wait_quad(act, att_ok, front + (-1))
                    act.activation(work[:, E_, :], bank[2][:], ACT.Exp, scale=2.0).then_inc(exp_ok, 1)
                    wait_quad(act, msg_done, front)
                    wait_quad(act, nmp_done, front + (-2))
                    act.activation(msg[:, p, :], bank[3][:], ACT.Relu).then_inc(msg_ok, 1)

            run_steps(act, step)

            def step(n):
                before = n + (-1)
                if n.exists():
                    wait_quad(act, t_turned, n)
                    wait_quad(act, t_hid_done, n + (-2))
                    act.activation(t_ynT[:, n.par, :], bank[n.par][:], ACT.Copy).then_inc(t_ynT_ok, 1)
                if before.exists():
                    p = before.par
                    wait_quad(act, t_hid_done, before)
                    wait_quad(act, t_out_done, before + (-2))
                    for t in range(TG):
                        cols = slice(t * 128, t * 128 + 128)
                        last = act.activation(t_hid[0:HID, p, cols], bank[2 + p][0:HID, cols], ACT.Relu,
                                              bias=t_w1[0:HID, p, t, HID:HID + 1])
                    last.then_inc(t_hid_ok, 1)

            run_groups(act, step)

        @block.vector
        def _(dve):
            chain = [0]

            def link(ins):
                chain[0] += 1
                ins.then_inc(dve_setup, 1)
                dve.wait_ge(dve_setup, chain[0])

            def layer_stats(q, k, src, stats_ok, mv_ok, nv_ok):
                p = q.par
                for g in range(QG):
                    last = dve.bn_stats(stats[:, p, g, :], src[:, p, g, :])
                last.then_inc(stats_ok, 1)
                pass_quad(dve, stats_ok, q, dve_passed)
                for g in range(QG):
                    last = dve.bn_aggr(mv[:, p, g, :], stats[:, p, g, :])
                last.then_inc(mv_ok, 1)
                wait_quad(dve, mv_ok, q)
                dve.tensor_scalar(negm[:, k + p, :], mv[:, p, :, 0], -1.0, None, ALU.mult)
                dve.tensor_scalar(veps[:, k + p, :], mv[:, p, :, 1], EPS, None, ALU.add).then_inc(nv_ok, 1)

            link(dve.memset(fill_row, 0.0))
            link(dve.memset(fill_row[:, R_ID:R_ID + 1].bitcast(i32), NO_TOKEN))
            dve.sem_inc(template, 1)
            dve.wait_ge(bn_loaded, 16 * BN_VECTORS)
            dve.tensor_scalar(vec[:, V_V1:V_V1 + 1], vec[:, V_V1:V_V1 + 1], EPS, None, ALU.add)
            dve.tensor_scalar(vec[:, V_V2:V_V2 + 1], vec[:, V_V2:V_V2 + 1], EPS, None, ALU.add).then_inc(bn_vec, 1)
            dve.wait_ge(bn_pow, 1)
            for s, g, v, m, b, t in ((V_S1, V_G1, V_V1, V_M1, V_B1, V_T1), (V_S2, V_G2, V_V2, V_M2, V_B2, V_T2)):
                link(dve.tensor_tensor(vec[:, s:s + 1], vec[:, g:g + 1], vec[:, v:v + 1], ALU.mult))
                link(dve.tensor_tensor(vec[:, t:t + 1], vec[:, m:m + 1], vec[:, s:s + 1], ALU.mult))
                link(dve.tensor_tensor(vec[:, t:t + 1], vec[:, b:b + 1], vec[:, t:t + 1], ALU.subtract))
            dve.wait_ge(w_loaded, 16 * 9)
            dve.tensor_scalar(c2_raw, c2_raw, vec[:, V_S2:V_S2 + 1], None, ALU.mult)
            dve.tensor_scalar(c1_raw, c1_raw, vec[:, V_S1:V_S1 + 1], None, ALU.mult).then_inc(bn_scaled, 1)
            dve.wait_ge(v_loaded, 16 * VECTORS)
            link(dve.tensor_tensor(vec[:, V_HR:V_HR + 2], vec[:, V_IHR:V_IHR + 2], vec[:, V_HHR:V_HHR + 2], ALU.add))
            dve.tensor_scalar(vec[:, V_HR:V_HR + 2], vec[:, V_HR:V_HR + 2], 0.5, None, ALU.mult)
            dve.tensor_scalar(vec[:, V_HN:V_HN + 1], vec[:, V_HHN:V_HHN + 1], 0.5, None, ALU.mult
                              ).then_inc(bn_vec, 1)
            wait_dma(dve, x_loaded, Quad(0))
            layer_stats(Quad(0), 0, x_nat, ln1_stats, ln1_mv, ln1_nv)
            for g in range(8):
                dve.wait_ge(w_hi, g + 1)
                lo, hi = g * 512, min(g * 512 + 512, WT_COLS)
                dve.tensor_tensor(wt_lo[:, lo:hi], bank[g][:, 0:hi - lo], f(wt_hi[:, lo:hi]), ALU.subtract
                                  ).then_inc(w_lo, 1)
            link(dve.memset(bmsg_parts[:], 0.0))
            src = bm_raw
            for k, r in enumerate((0, 32, 64)):
                link(dve.tensor_copy(bm_p[:], src))
                link(dve.tensor_copy(bmsg_parts[r:r + 1], bm_p[r:r + 1]))
                if k < 2:
                    link(dve.tensor_tensor(bm_rest, src, bm_p[:], ALU.subtract))
                    src = bm_rest
            link(dve.transpose(b1_turned[:], b1_nat[:]))
            dve.wait_ge(zeroed, 1)
            link(dve.tensor_copy(w1b1[0:HID, :, HID], b1_turned[:]))
            dve.sem_inc(bmsg_ok, 1)
            dve.wait_ge(state_zero, 1)

            def then(q, k, ins):
                ins.then_inc(route[k], 1)
                wait_quad(dve, route[k], q)

            counts = ranked_counts[:, QG * EXPERTS:(QG + 1) * EXPERTS]
            ranks = by_graph(ranked_counts[:, 0:QG * EXPERTS])

            def open_tiles(q):
                wait_quad(dve, counted, q)
                dve.tensor_copy(ranked_counts[:], bank[1][:, 0:(QG + 1) * EXPERTS]).then_inc(ranks_kept, 1)
                wait_quad(dve, ranks_kept, q)
                then(q, 0, dve.tensor_tensor(over[:], counts, free[:], ALU.subtract))
                dve.tensor_scalar(opens[:], over[:], 0.0, None, ALU.is_gt)
                then(q, 1, dve.tensor_tensor(past[:], over_graphs(over[:]), bounds[:].rearrange(
                    "p (g o) -> p g o", o=1).to_broadcast([128, TOK // TILE, EXPERTS]), ALU.is_gt))
                dve.tensor_tensor(in_open[:], ranks, over_graphs(free[:]), ALU.is_lt)
                then(q, 2, dve.tensor_reduce(new_base[:], past[:].rearrange("p k e -> p e k"), AX.X, ALU.add))
                dve.tensor_scalar(news[:], new_base[:], float(TILE), None, ALU.mult)
                then(q, 3, dve.tensor_scalar(run[:, 0, SHIFT:], new_base[:], float(TILE), None, ALU.mult))
                at = 0
                for k in range(5):
                    then(q, 4 + k, dve.tensor_tensor(run[:, 1 - at, SHIFT:], run[:, at, SHIFT:],
                                                     run[:, at, SHIFT - (1 << k):SHIFT + EXPERTS - (1 << k)],
                                                     ALU.add))
                    at = 1 - at
                then(q, 9, dve.tensor_scalar(new_end[:], run[:, at, SHIFT:], opened[:], None, ALU.add))

            def give_slots(q):
                dve.tensor_copy(opened[:], new_end[:, EXPERTS - 1:EXPERTS])
                dve.tensor_tensor(run[:, 0, SHIFT:], new_end[:], end[:], ALU.subtract)
                then(q, 10, dve.tensor_tensor(new_base[:], new_end[:], news[:], ALU.subtract))
                dve.tensor_tensor(off_new[:], new_base[:], free[:], ALU.subtract)
                dve.tensor_tensor(off_open[:], end[:], new_base[:], ALU.subtract)
                for h in range(HALVES):
                    last = dve.tensor_scalar(tile_cmp[:, h, :], new_base[:], tile_start[:, h:h + 1], None,
                                             ALU.is_le)
                then(q, 11, last)
                dve.tensor_tensor(in_open[:], in_open[:], over_graphs(off_open[:]), ALU.mult)
                dve.tensor_tensor(slot_e[:], ranks, over_graphs(off_new[:]), ALU.add)
                dve.tensor_tensor(run[:, 0, SHIFT:], run[:, 0, SHIFT:], opens[:], ALU.mult)
                dve.tensor_tensor(free[:], news[:], over[:], ALU.subtract)
                dve.tensor_scalar(token[:], token[:], float(TOK), None, ALU.add)
                for h in range(HALVES):
                    last = dve.scalar_tensor_tensor(out=tile_cmp[:, h, :], in0=new_end[:],
                                                    scalar=tile_start[:, h:h + 1], in1=tile_cmp[:, h, :],
                                                    op0=ALU.is_gt, op1=ALU.mult)
                then(q, 12, last)
                dve.tensor_tensor(slot_e[:], slot_e[:], in_open[:], ALU.add)
                dve.tensor_tensor(end[:], end[:], run[:, 0, SHIFT:], ALU.add)
                wait_scatter(dve, q + (-2))
                dve.tensor_copy(row[:, q.par, :, R_ID].bitcast(i32), token[:])
                then(q, 13, dve.tensor_tensor(has_tile[:], has_tile[:], tile_cmp[:], ALU.add))
                then(q, 14, dve.tensor_tensor(slot_e[:], slot_e[:], onehot[:], ALU.mult))
                then(q, 15, dve.tensor_reduce(slot_f[:], slot_e[:], AX.X, ALU.add))
                dve.tensor_copy(slot[:, q.par, :], slot_f[:]).then_inc(slots_ok, 1)

            def step(q):
                ahead, front, back, old = q + 2, q + 1, q + (-1), q + (-2)
                if old.exists():
                    open_tiles(old)
                if back.exists():
                    wait_quad(dve, gruT_done, back)
                    wait_scatter(dve, back + (-2))
                    dve.tensor_tensor(row[:, back.par, :, R_X:R_X + D], by_graph(bank[3][:]),
                                      x_keep[:, back.par, :, :], ALU.add).then_inc(x2_ok, 1)
                if q.exists():
                    wait_quad(dve, nmp_hi_ok, q)
                    dve.tensor_tensor(nmp_lo[:, q.par, :], bank[2][:], f(nmp_hi[:, q.par, :]),
                                      ALU.subtract).then_inc(nmp_lo_ok, 1)
                if back.exists():
                    wait_quad(dve, x2_ok, back)
                    layer_stats(back, 2, row[:, :, :, R_X:R_X + D], ln2_stats, ln2_mv, ln2_nv)
                if old.exists():
                    give_slots(old)
                if q.exists():
                    wait_quad(dve, conv2_done, q)
                    dve.scalar_tensor_tensor(out=work[:, T_, :], in0=bank[0][:], scalar=vec[:, V_T2:V_T2 + 1],
                                             in1=xnT[:, q.par, :], op0=ALU.add, op1=ALU.add).then_inc(xc_t, 1)
                if front.exists():
                    p = front.par
                    wait_quad(dve, xnT_full, front)
                    wait_quad(dve, gate_n_i, front + (-2))
                    dve.tensor_copy(xnT_hi[:, p, :], xnT[:, p, :]).then_inc(xnT_hi_ok, 1)
                if q.exists():
                    wait_quad(dve, xc_hi_ok, q)
                    dve.scalar_tensor_tensor(out=xc_lo[:, q.par, :], in0=work[:, T_, :], scalar=0.0,
                                             in1=f(xc_hi[:, q.par, :]), op0=ALU.max, op1=ALU.subtract
                                             ).then_inc(xc_lo_ok, 1)
                if back.exists():
                    wait_quad(dve, yn_hi_ok, back)
                    dve.tensor_tensor(yn_lo[:], bank[1][:], f(yn_hi[:]), ALU.subtract).then_inc(yn_lo_ok, 1)
                if ahead.exists():
                    wait_dma(dve, x_loaded, ahead)
                    layer_stats(ahead, 0, x_nat, ln1_stats, ln1_mv, ln1_nv)
                if front.exists():
                    wait_quad(dve, h1_full, front)
                    wait_quad(dve, conv2_done, front + (-2))
                    dve.tensor_copy(h1_hi[:, p, :, PAD:PAD + NODES], by_graph(h1[:, p, :])).then_inc(h1_hi_ok, 1)
                    wait_quad(dve, se_sq, front)
                    dve.tensor_copy(dist_l[0:3, p, :], dist_r[0:3, p, :]).then_inc(se_l, 1)
                if q.exists():
                    wait_quad(dve, tr_ok, q)
                    wait_quad(dve, gh_ok, q)
                    dve.scalar_tensor_tensor(out=work[:, W_, :], in0=work[:, TR, :], scalar=1.0,
                                             in1=work[:, GH, :], op0=ALU.add, op1=ALU.mult).then_inc(rgh_ok, 1)
                    wait_quad(dve, rgh_ok, q)
                    wait_quad(dve, gate_n_i, q)
                    dve.tensor_tensor(work[:, W_, :], bank[6][:], work[:, W_, :], ALU.add).then_inc(w_ok, 1)
                if back.exists():
                    logit = by_graph(bank[1][:, 0:QG * EXPERTS])
                    wait_quad(dve, logit_done, back)
                    dve.tensor_reduce(lmax[:], logit, AX.X, ALU.max).then_inc(am_max, 1)
                    wait_quad(dve, am_max, back)
                    dve.tensor_tensor(ranked[:], logit, lmax[:].rearrange("p (g o) -> p g o", o=1)
                                      .to_broadcast([128, QG, EXPERTS]), ALU.is_equal).then_inc(am_eq, 1)
                    wait_quad(dve, am_eq, back)
                    dve.tensor_tensor(ranked[:], ranked[:], over_graphs(rank[:]), ALU.mult).then_inc(am_rank, 1)
                    wait_quad(dve, am_rank, back)
                    dve.tensor_reduce(first[:], ranked[:], AX.X, ALU.max).then_inc(am_first, 1)
                    wait_quad(dve, am_first, back)
                    dve.tensor_tensor(onehot[:], ranked[:], first[:].rearrange("p (g o) -> p g o", o=1)
                                      .to_broadcast([128, QG, EXPERTS]), ALU.is_equal).then_inc(onehot_ok, 1)
                if q.exists():
                    wait_quad(dve, gru_d, q)
                    wait_quad(dve, tz_ok, q)
                    dve.scalar_tensor_tensor(out=work[:, DE, :], in0=work[:, TZ, :], scalar=1.0,
                                             in1=work[:, DE, :], op0=ALU.add, op1=ALU.mult).then_inc(gru_e, 1)
                    wait_quad(dve, gru_e, q)
                    wait_quad(dve, gruT_done, q + (-1))
                    dve.scalar_tensor_tensor(out=work[:, F_, :], in0=work[:, DE, :], scalar=0.5,
                                             in1=work[:, N_, :], op0=ALU.mult, op1=ALU.add).then_inc(gru_f, 1)

            run_steps(dve, step)

            last_quad = Quad(QUADS - 1)
            wait_quad(dve, slots_ok, last_quad)
            dve.tensor_tensor(tile_cmp[:], has_tile[:], expert_no[:].rearrange("p (o e) -> p o e", o=1)
                              .to_broadcast([128, HALVES, EXPERTS]), ALU.mult).then_inc(table_sum, 1)
            dve.wait_ge(table_sum, 1)
            dve.tensor_reduce(tile_e[:], tile_cmp[:], AX.X, ALU.add).then_inc(table_sum, 1)
            dve.wait_ge(table_row, 1)
            dve.tensor_copy(tile_expert[:], bank[0][0:1, 0:HALVES * 128]).then_inc(table_ok, 1)
            dve.wait_ge(table_ok, 1)
            dve.wait_ge(e_loaded, 48)

            def step(n):
                done = n + (-2)
                if n.exists():
                    p = n.par
                    pass_quad(dve, t_hid_ok, n + (-2), dve_passed)
                    experts = [dve.value_load(tile_expert[0:1, bass.ds(TG * n.index() + t, 1)], min_val=0,
                                              max_val=EXPERTS - 1) for t in range(TG)]
                    for t, e in enumerate(experts):
                        last = dve.tensor_copy(t_w1[:, p, t, :],
                                               w1b1[:, bass.ds(e, 1), :].rearrange("p o h -> p (o h)"))
                    last.then_inc(t_w1_ok, 1)
                if done.exists():
                    p = done.par
                    wait_quad(dve, t_out_done, done)
                    wait_tiles_scattered(dve, done + (-2))
                    dve.tensor_copy(ids[:, done.lap, :], rows_in[:, done.lap, :, R_ID].bitcast(i32))
                    dve.scalar_tensor_tensor(out=t_out[:, p, :, :], in0=by_graph(bank[4 + p][:]), scalar=0.0,
                                             in1=rows_in[:, done.lap, :, R_X:R_X + D], op0=ALU.max, op1=ALU.add
                                             ).then_inc(t_out_ok, 1)

            run_groups(dve, step)

        @block.tensor
        def _(pe):
            def raw(i):
                if i < TAPS:
                    return c2_raw.rearrange("p (i k) -> p i k", k=TAPS)[:, :, i]
                if i == W_CONV1:
                    return c1_raw
                if i < W_IH_NMP:
                    return ih_raw[:, (i - W_IH_CONV) * 256:(i - W_IH_CONV) * 256 + 128]
                if i < W_HH:
                    return ih_raw[:, (i - W_IH_NMP) * 256 + 128:(i - W_IH_NMP) * 256 + 256]
                if i < W_MSG:
                    return hh_raw[:, (i - W_HH) * 128:(i - W_HH) * 128 + 128]
                return msg_raw

            pe.wait_ge(pool_setup, 7)
            pe.wait_ge(w_loaded, 16 * 9)
            pe.wait_ge(bn_scaled, 1)
            for g in range(7):
                for k in range(4):
                    last = pe.transpose(bank[g][:, k * 128:k * 128 + 128], raw(4 * g + k), ident[:])
                last.then_inc(w_turned, 1)
            pe.transpose(bank[7][:, 0:EXPERTS], rout_raw, ident[0:EXPERTS, 0:EXPERTS])
            pe.transpose(bank[7][:, EXPERTS:EXPERTS + SE_ROWS], se_raw, ident[0:SE_ROWS, 0:SE_ROWS]
                         ).then_inc(w_turned, 1)
            pe.wait_ge(w_lo, 8)

            def split3(dst, lo_col, cols, hi, lo, start, stop):
                wh, wl = wt_hi[:, lo_col:lo_col + cols], wt_lo[:, lo_col:lo_col + cols]
                pe.matmul(dst, wh, hi, start=start, stop=False)
                pe.matmul(dst, wh, lo, start=False, stop=False)
                return pe.matmul(dst, wl, hi, start=False, stop=stop)

            def block_of(i, dst, hi, lo, start, stop):
                return split3(dst, i * 128, 128, hi, lo, start, stop)

            def turn(dst, src):
                for g in range(QG):
                    last = pe.transpose(dst[:, g * 128:g * 128 + 128], src(g), ident[:])
                return last

            def conv2(q, taps):
                for k in taps:
                    last = block_of(W_CONV2 + k, bank[0][:], h1_hi[:, q.par, :, k:k + NODES],
                                    h1_lo[:, q.par, :, k:k + NODES], k == 0, k == TAPS - 1)
                return last

            def step(q):
                front, back, old = q + 1, q + (-1), q + (-2)
                if q.exists():
                    wait_quad(pe, h1_hi_ok, q)
                    wait_quad(pe, h1_lo_ok, q)
                    wait_quad(pe, xc_t, back)
                    conv2(q, range(0, 2))
                if old.exists():
                    if old.n == 0 and old.it is None:
                        pe.wait_ge(state_zero, 1)
                    wait_quad(pe, onehot_ok, old)
                    ranks = bank[1][:, 0:QG * EXPERTS]
                    pe.matmul(ranks, earlier[:], onehot[:].rearrange("p g e -> p (g e)"), start=True, stop=False)
                    for g in range(QG - 1):
                        later = QG - 1 - g
                        pe.matmul(bank[1][:, (g + 1) * EXPERTS:QG * EXPERTS].rearrange("p (g e) -> p g e", g=later),
                                  ones_bf[:], onehot[:, g:g + 1, :].to_broadcast([128, later, EXPERTS]),
                                  start=False, stop=g == QG - 2)
                    for g in range(QG):
                        last = pe.matmul(bank[1][:, QG * EXPERTS:(QG + 1) * EXPERTS], ones_bf[:], onehot[:, g, :],
                                         start=g == 0, stop=g == QG - 1)
                    last.then_inc(counted, 1)
                if q.exists():
                    conv2(q, range(2, 5))
                    wait_quad(pe, exp_ok, q)
                    wait_quad(pe, msg_ok, q)
                    wait_quad(pe, att_ok, q)
                    for g in range(QG):
                        cols = slice(g * 128, g * 128 + 128)
                        last = pe.matmul(bank[2][:, cols], msg[:, q.par, cols], att[:, q.par, cols],
                                         start=True, stop=True)
                    last.then_inc(nmp_done, 1)
                if back.exists():
                    wait_quad(pe, gru_f, back)
                    if q.exists():
                        wait_quad(pe, msg_ok, q)
                    turn(bank[3], lambda g: work[:, F_, g * 128:g * 128 + 128]).then_inc(gruT_done, 1)
                if q.exists():
                    conv2(q, range(5, TAPS)).then_inc(conv2_done, 1)
                if front.exists():
                    p = front.par
                    wait_quad(pe, xn_ready, front)
                    if q.exists():
                        wait_quad(pe, nmp_lo_ok, q)
                    turn(bank[2], lambda g: xn[:, p, g, :]).then_inc(xnT_done, 1)
                    wait_dma(pe, adj_loaded, front)
                    if back.exists():
                        wait_quad(pe, x2_ok, back)
                    turn(bank[3], lambda g: adj_nat[:, p, g, :]).then_inc(adjT_done, 1)
                if back.exists():
                    wait_quad(pe, yn_ready, back)
                    wait_quad(pe, ranks_kept, old)
                    turn(bank[1], lambda g: row[:, back.par, g, R_N:R_N + D]).then_inc(ynT_done, 1)
                if q.exists():
                    s = q.par
                    wait_quad(pe, w_ok, back)
                    wait_quad(pe, tz_ok, back)
                    xh, xl, nh, nl = xnT_hi[:, s, :], xnT_lo[:, s, :], nmp_hi[:, s, :], nmp_lo[:, s, :]
                    block_of(W_HH + 2, bank[7][:], xh, xl, True, True).then_inc(gate_n_h, 1)
                    wait_quad(pe, nmp_hi_ok, q)
                    wait_quad(pe, nmp_lo_ok, q)
                    for i in range(2):
                        block_of(W_HH + i, bank[4 + i][:], xh, xl, True, False)
                        block_of(W_IH_NMP + i, bank[4 + i][:], nh, nl, False, False)
                    block_of(W_IH_NMP + 2, bank[6][:], nh, nl, True, False)
                if front.exists():
                    wait_quad(pe, xnT_hi_ok, front)
                    wait_quad(pe, xnT_lo_ok, front)
                    block_of(W_CONV1, bank[2][:], xnT_hi[:, p, :], xnT_lo[:, p, :], True, True
                             ).then_inc(conv1_done, 1)
                    wait_quad(pe, adjT_ok, front)
                    split3(bank[3][0:SE_ROWS, :], SE_COL, SE_ROWS, xnT_hi[:, p, :], xnT_lo[:, p, :], True, True
                           ).then_inc(se_done, 1)
                if back.exists():
                    wait_quad(pe, yn_hi_ok, back)
                    wait_quad(pe, yn_lo_ok, back)
                    split3(bank[1][0:EXPERTS, :], ROUTER_COL, EXPERTS, yn_hi[:], yn_lo[:], True, True
                           ).then_inc(router_done, 1)
                if q.exists():
                    wait_quad(pe, xc_hi_ok, q)
                    wait_quad(pe, xc_lo_ok, q)
                    for i, done in enumerate((gate_r, gate_z, gate_n_i)):
                        block_of(W_IH_CONV + i, bank[4 + i][:], xc_hi[:, s, :], xc_lo[:, s, :], False, True
                                 ).then_inc(done, 1)
                if back.exists():
                    pass_quad(pe, logitT_ok, back, pe_passed)
                    for g in range(QG):
                        last = pe.transpose(bank[1][:, g * EXPERTS:(g + 1) * EXPERTS],
                                            logitT[:, g * 128:g * 128 + 128], ident[0:EXPERTS, 0:EXPERTS])
                    last.then_inc(logit_done, 1)
                if front.exists():
                    wait_quad(pe, h1_full, front)
                    wait_quad(pe, se_sq, front)
                    wait_quad(pe, se_l, front)
                    for g in range(QG):
                        cols = slice(g * 128, g * 128 + 128)
                        last = pe.matmul(bank[2][:, cols], dist_l[:, p, cols], dist_r[:, p, cols],
                                         start=True, stop=True)
                    last.then_inc(dist_done, 1)
                    if front.n == 0 and front.it is None:
                        pe.wait_ge(bmsg_ok, 1)
                    for g in range(QG):
                        pe.matmul(bank[3][:, g * 128:g * 128 + 128], ones_bf[0:65, :], bmsg_parts[:],
                                  start=True, stop=False)
                        last = pe.matmul(bank[3][:, g * 128:g * 128 + 128], xnT[:, p, g * 128:g * 128 + 128],
                                         wmsg[:], start=False, stop=True)
                    last.then_inc(msg_done, 1)

            run_steps(pe, step)

            pe.wait_ge(table_sum, 2)
            for h in range(HALVES):
                last = pe.matmul(bank[0][0:1, h * 128:h * 128 + 128], tile_e[:, h:h + 1], ident[:],
                                 start=True, stop=True)
            last.then_inc(table_row, 1)
            pe.wait_ge(table_ok, 1)
            pe.wait_ge(e_loaded, 48)

            def step(n):
                before, done = n + (-1), n + (-2)
                if n.exists():
                    wait_dma(pe, rows_loaded, n)
                    wait_quad(pe, t_ynT_ok, n + (-2))
                    turn(bank[n.par], lambda t: rows_in[:, n.lap, t, R_N:R_N + D]).then_inc(t_turned, 1)
                if before.exists():
                    p = before.par
                    wait_quad(pe, t_ynT_ok, before)
                    wait_quad(pe, t_w1_ok, before)
                    wait_quad(pe, t_hid_ok, before + (-2))
                    for t in range(TG):
                        cols = slice(t * 128, t * 128 + 128)
                        last = pe.matmul(bank[2 + p][0:HID, cols], t_w1[:, p, t, 0:HID], t_ynT[:, p, cols],
                                         start=True, stop=True)
                    last.then_inc(t_hid_done, 1)
                if done.exists():
                    p = done.par
                    wait_quad(pe, t_out_ok, done + (-2))
                    pass_quad(pe, t_hid_ok, done, pe_passed)
                    for t in range(TG):
                        e = pe.value_load(tile_expert[0:1, bass.ds(TG * done.index() + t, 1)], min_val=0,
                                          max_val=EXPERTS - 1)
                        last = pe.matmul(bank[4 + p][:, t * 128:t * 128 + 128],
                                         t_hid[:, p, t * 128:t * 128 + 128], w2b2[:, bass.ds(e * D, D)],
                                         start=True, stop=True)
                    last.then_inc(t_out_done, 1)

            run_groups(pe, step)


def kernel(**inputs):
    import concourse.bacc as bacc
    from concourse.bass_utils import run_bass_kernel_spmd

    nc = bacc.Bacc("TRN2", target_bir_lowering=False, num_devices=1)
    arrays, args = {}, {}
    for name, value in inputs.items():
        value = np.ascontiguousarray(value)
        arrays[f"in_{name}"] = value
        args[name] = nc.dram_tensor(f"in_{name}", value.shape, mybir.dt.from_np(value.dtype),
                                    kind="ExternalInput").ap()
    out = nc.dram_tensor("out", (GRAPHS, NODES, D), mybir.dt.float32, kind="ExternalOutput").ap()
    program(nc, args, out)
    result = run_bass_kernel_spmd(nc, [arrays], core_ids=[0])
    return np.asarray(result.results[0]["out"])
```

```python
from contextlib import ExitStack

import numpy as np
import concourse.bass as bass
from concourse import mybir

GRAPHS, NODES, D = 128, 128, 128
TAPS = 17
PAD = TAPS // 2
EXPERTS, HID = 32, 32
EPS = 1e-5
QG = 4
QUADS = GRAPHS // QG
TOK = QG * NODES
PADDED = NODES + 2 * PAD
TOKENS = GRAPHS * NODES
TILE = 128
TILES = (TOKENS + EXPERTS * (TILE - 1)) // TILE
TILES += -TILES % 8
FILLS = 16
R_X, R_N, R_ID, ROW = 0, D, 2 * D, 2 * D + 4
NO_TOKEN = 1 << 20
TG = 4
GROUPS = TILES // TG
LOOP_FIRST, LOOP_LAST = 4, 29
BN_VECTORS, BIASES, SMALL_ONES = 8, 6, 5
BANKS = (5, 6, 7, 4, 2, 3, 0, 1)
W_CONV2, W_CONV1 = 0, TAPS
W_IH_CONV = TAPS + 1
W_IH_NMP = W_IH_CONV + 3
W_HH = W_IH_NMP + 3
W_MSG = W_HH + 3
W_SMALL = W_MSG + 1
SE_COL = W_SMALL * 128
SE_ROWS = 67
WT_COLS = SE_COL + SE_ROWS


class Step:

    def __init__(self, n, it=None):
        self.n, self.it, self.par, self.lap = n, it, n % 2, n % self.every

    def __add__(self, k):
        return type(self)(self.n + k, self.it)

    def exists(self):
        return self.it is not None or 0 <= self.n < self.count

    def index(self):
        return self.n if self.it is None else self.every * self.it + self.n

    def events(self):
        return self.n + 1 if self.it is None else self.every * self.it + (self.n + 1)

    def loads(self):
        n = self.n // self.every + 1
        return 16 * n if self.it is None else 16 * self.it + 16 * n


class Quad(Step):
    count, every = QUADS, 2


class Group(Step):
    count, every = GROUPS, 4


def wait_quad(eng, sem, q):
    if q.n >= 0:
        eng.wait_ge(sem, q.events())


def pass_quad(eng, sem, q, passed):
    if q.n >= 0:
        eng.wait_ge(sem, q.events())
        eng.sem_inc(passed, 1)


def wait_dma(eng, sems, q):
    if q.n >= 0:
        eng.wait_ge(sems[q.lap], q.loads())


def run_steps(eng, step):
    for n in range(-1, LOOP_FIRST):
        step(Quad(n))
    with eng.Fori(0, (LOOP_LAST - LOOP_FIRST + 1) // 2) as it:
        for k in range(2):
            step(Quad(LOOP_FIRST + k, it))
    for n in range(LOOP_LAST + 1, QUADS + 2):
        step(Quad(n))


def run_groups(eng, step):
    for n in range(4):
        step(Group(n))
    with eng.Fori(0, GROUPS // 4 - 1) as it:
        for k in range(4):
            step(Group(4 + k, it))
    for n in range(GROUPS, GROUPS + 2):
        step(Group(n))


def program(nc, a, out):
    f32, f32r, bf16 = mybir.dt.float32, mybir.dt.float32r, mybir.dt.bfloat16
    i32, u32 = mybir.dt.int32, mybir.dt.uint32
    ALU, ACT, AX = mybir.AluOpType, mybir.ActivationFunctionType, mybir.AxisListType
    ctx = ExitStack()

    def sb(name, shape, dt=f32):
        return ctx.enter_context(nc.sbuf_tensor(name, shape, dt))

    def sem(name):
        return ctx.enter_context(nc.semaphore(name))

    def sems(name, n):
        return [sem(f"{name}{i}") for i in range(n)]

    with ctx:
        x_v = a["x"].rearrange("(q g) t d -> q t g d", g=QG)
        adj_v = a["adj"].rearrange("(q g) t d -> q t g d", g=QG)
        out_rows = out.rearrange("b t d -> (b t) d")
        sorted_rows = nc.dram_tensor("sorted_rows", [TILES * TILE, ROW], f32).ap()
        groups_v = sorted_rows.rearrange("(n t p) c -> n p t c", t=TG, p=TILE)

        wt_hi = sb("wt_hi", [128, WT_COLS], f32r)
        wt_lo = sb("wt_lo", [128, WT_COLS], f32r)
        wmsg = sb("wmsg", [128, 128])
        w1b1 = sb("w1b1", [128, EXPERTS, HID + 1])
        b1_nat, b1_turned = sb("b1_nat", [EXPERTS, HID]), sb("b1_turned", [HID, EXPERTS])
        w2b2 = sb("w2b2", [HID + 1, EXPERTS * D])
        bmsg = sb("bmsg", [128, D])
        ones_bf = sb("ones_bf", [128, 128], bf16)
        earlier = sb("earlier", [128, 128], bf16)
        ident = sb("ident", [128, 128])
        rank = sb("rank", [128, EXPERTS])
        expert_no = sb("expert_no", [128, EXPERTS])
        minus_half = sb("minus_half", [128, QG])
        (V_G1, V_B1, V_M1, V_V1, V_G2, V_B2, V_M2, V_V2, V_IHR, V_IHZ, V_IHN, V_HHR, V_HHZ, V_HHN,
         V_S1, V_S2, V_T1, V_T2, V_HR, V_HZ, V_HN) = range(21)
        vec = sb("vec", [128, 21])
        bse = sb("bse", [SE_ROWS, 1])
        wrout = sb("wrout", [128, EXPERTS])
        brout = sb("brout", [128, EXPERTS])

        x_nat = sb("x_nat", [128, 2, QG, D])
        x_keep = sb("x_keep", [128, 2, QG, D])
        adj_nat = sb("adj_nat", [128, 2, QG, NODES])
        xn = sb("xn", [128, 2, QG, D])
        xnT = sb("xnT", [128, 2, TOK])
        xnT_hi = sb("xnT_hi", [128, 2, TOK], f32r)
        xnT_lo = sb("xnT_lo", [128, 2, TOK], f32r)
        adjT = sb("adjT", [128, 2, TOK])
        h1 = sb("h1", [128, 2, TOK])
        h1_hi = sb("h1_hi", [128, 2, QG, PADDED], f32r)
        h1_lo = sb("h1_lo", [128, 2, QG, PADDED], f32r)
        dist_l = sb("dist_l", [SE_ROWS, 2, TOK])
        dist_r = sb("dist_r", [SE_ROWS, 2, TOK])
        msg = sb("msg", [128, 2, TOK])
        att = sb("att", [128, 2, TOK])
        nmp_hi = sb("nmp_hi", [128, 2, TOK], f32r)
        nmp_lo = sb("nmp_lo", [128, 2, TOK], f32r)
        xc_hi = sb("xc_hi", [128, 2, TOK], f32r)
        xc_lo = sb("xc_lo", [128, 2, TOK], f32r)
        row = sb("row", [128, 4, QG, ROW])
        ynT = sb("ynT", [128, TOK])
        work = sb("work", [128, 9, TOK])
        (E_, T_, GH, TR, TZ, W_, N_, DE, F_) = range(9)
        logits = sb("logits", [128, QG, EXPERTS])
        lmax = sb("lmax", [128, QG])
        ranked = sb("ranked", [128, QG, EXPERTS])
        first = sb("first", [128, QG])
        onehot = sb("onehot", [128, QG, EXPERTS], bf16)
        stats = sb("stats", [128, 2, QG, 6])
        mv = sb("mv", [128, 2, QG, 2])
        negm = sb("negm", [128, 4, QG])
        veps = sb("veps", [128, 4, QG])
        rstd = sb("rstd", [128, 4, QG])

        free = sb("free", [128, EXPERTS])
        end = sb("end", [128, EXPERTS])
        opened = sb("opened", [128, 1])
        ranked_counts = sb("ranked_counts", [128, (QG + 1) * EXPERTS])
        bounds = sb("bounds", [128, TOK // TILE])
        past = sb("past", [128, TOK // TILE, EXPERTS])
        over = sb("over", [128, EXPERTS])
        opens = sb("opens", [128, EXPERTS])
        news = sb("news", [128, EXPERTS])
        SHIFT = EXPERTS // 2
        run = sb("run", [128, 2, SHIFT + EXPERTS])
        new_end = sb("new_end", [128, EXPERTS])
        new_base = sb("new_base", [128, EXPERTS])
        off_new = sb("off_new", [128, EXPERTS])
        off_open = sb("off_open", [128, EXPERTS])
        slot_e = sb("slot_e", [128, QG, EXPERTS])
        in_open = sb("in_open", [128, QG, EXPERTS])
        slot_f = sb("slot_f", [128, QG])
        slot = sb("slot", [128, 2, QG], i32)
        token = sb("token", [128, QG])
        HALVES = -(-TILES // 128)
        tile_start = sb("tile_start", [128, HALVES])
        has_tile = sb("has_tile", [128, HALVES, EXPERTS])
        tile_cmp = sb("tile_cmp", [128, HALVES, EXPERTS])
        tile_e = sb("tile_e", [128, HALVES])
        tile_expert = sb("tile_expert", [1, HALVES * 128], i32)

        rows_in = row
        ids = sb("ids", [128, 4, TG], i32)
        t_ynT = xnT
        t_w1 = sb("t_w1", [128, 2, TG, HID + 1])
        t_hid = sb("t_hid", [HID + 1, 2, TOK])
        t_out = xn

        flat = work[:, :, :].rearrange("p a n -> p (a n)")
        c2_raw = flat[:, 0:2176]
        ih_raw = flat[:, 2176:2944]
        hh_raw = flat[:, 2944:3328]
        c1_raw = flat[:, 3328:3456]
        msg_raw = flat[:, 3456:3584]
        rout_raw = flat[0:EXPERTS, 3584:3712]
        se_raw = flat[0:SE_ROWS, 3712:3840]
        fill_row = sb("fill_row", [128, ROW])[:, :]
        ints = sb("ints", [128, EXPERTS], i32)

        bank = [ctx.enter_context(nc.psum_tensor(f"bank{i}", [128, TOK], f32)) for i in range(8)]

        x_loaded, adj_loaded, scattered = sems("x_loaded", 2), sems("adj_loaded", 2), sems("scattered", 2)
        w_loaded, bn_loaded, b_loaded, bm_loaded, v_loaded, e_loaded, filled = (sem(n) for n in (
            "w_loaded", "bn_loaded", "b_loaded", "bm_loaded", "v_loaded", "e_loaded", "filled"))
        pool_setup, bn_pow, bn_vec, bn_scaled, dve_setup, state_zero, b1_placed, padded = (sem(n) for n in (
            "pool_setup", "bn_pow", "bn_vec", "bn_scaled", "dve_setup", "state_zero", "b1_placed", "padded"))
        zeroed, template, w_turned, w_hi, w_lo = (sem(n) for n in (
            "zeroed", "template", "w_turned", "w_hi_done", "w_lo_done"))
        (ln1_stats, ln1_mv, ln1_nv, ln1_rstd, xn_ready, x_kept, xnT_done, xnT_full, xnT_hi_ok, xnT_lo_ok,
         adjT_done, adjT_ok, conv1_done, h1_full, h1_hi_ok, h1_lo_ok, se_done, se_sq, se_l, msg_done, msg_sum,
         msg_ok, dist_done, exp_ok, att_ok, nmp_done, nmp_hi_ok, nmp_lo_ok, conv2_done, xc_t, xc_hi_ok,
         xc_lo_ok, gate_n_h, gate_r, gate_z, gate_n_i, gh_ok, tr_ok, tz_ok, rgh_ok, w_ok, n_ok, gru_d,
         gru_e, gru_f, gruT_done, x2_ok, ln2_stats, ln2_mv, ln2_nv, ln2_rstd, yn_ready, ynT_done,
         ynT_ok, logit_done, logits_ok, am_max, am_eq, am_rank, am_first,
         onehot_ok, counted, ranks_kept, slots_ok) = (
            sem(n) for n in """ln1_stats ln1_mv ln1_nv ln1_rstd xn_ready x_kept xnT_done xnT_full
            xnT_hi_ok xnT_lo_ok adjT_done adjT_ok conv1_done h1_full h1_hi_ok h1_lo_ok se_done se_sq
            se_l msg_done msg_sum msg_ok dist_done exp_ok att_ok nmp_done nmp_hi_ok nmp_lo_ok conv2_done xc_t
            xc_hi_ok xc_lo_ok gate_n_h gate_r gate_z gate_n_i gh_ok tr_ok tz_ok rgh_ok w_ok n_ok gru_d
            gru_e gru_f gruT_done x2_ok ln2_stats ln2_mv ln2_nv ln2_rstd yn_ready ynT_done ynT_ok
            logit_done logits_ok am_max am_eq am_rank am_first onehot_ok
            counted ranks_kept slots_ok""".split())
        ROUTE_STEPS = 16
        route = sems("route", ROUTE_STEPS)
        table_sum, table_row, table_ok = sem("table_sum"), sem("table_row"), sem("table_ok")
        rows_loaded, t_scattered = sems("rows_loaded", 4), sems("t_scattered", 4)
        (t_turned, t_ynT_ok, t_w1_ok, t_hid_done, t_hid_ok, t_out_done, t_out_ok) = (
            sem(n) for n in "t_turned t_ynT_ok t_w1_ok t_hid_done t_hid_ok t_out_done t_out_ok".split())
        dve_passed, pool_passed, pe_passed = sem("dve_passed"), sem("pool_passed"), sem("pe_passed")

        def f(ap):
            return ap.bitcast(f32)

        def by_graph(ap):
            return ap.rearrange("p (g n) -> p g n", g=QG)

        def over_graphs(ap):
            return ap.rearrange("p (o e) -> p o e", o=1).to_broadcast([128, QG, EXPERTS])

        def wait_scatter(eng, q):
            if q.n >= 0:
                eng.wait_ge(scattered[q.par], QG * q.loads())

        def wait_tiles_scattered(eng, n):
            if n.n >= 0:
                eng.wait_ge(t_scattered[n.lap], TG * n.loads())

        def experts_of(eng, regs, n):
            eng.load(regs, tile_expert[0:1, bass.ds(n.index() * TG, TG)])
            return [eng.snap(r, min_val=0, max_val=EXPERTS - 1) for r in regs]

        block = ctx.enter_context(nc.Block())

        @block.sync
        def _(sp):
            def load_x(q):
                sp.dma_start(x_nat[:, q.par, :, :], x_v[bass.ds(q.index(), 1)][0]).then_inc(x_loaded[q.par], 16)

            def load_adj(q):
                sp.dma_start(adj_nat[:, q.par, :, :], adj_v[bass.ds(q.index(), 1)][0]
                             ).then_inc(adj_loaded[q.par], 16)

            load_x(Quad(0))
            sp.dma_start(c2_raw, a["L0_gnn_conv2_w"].rearrange("o i k -> o (i k)")).then_inc(w_loaded, 16)
            sp.dma_start(c1_raw, a["L0_gnn_conv1_w"].rearrange("o i k -> o (i k)")).then_inc(w_loaded, 16)
            sp.dma_start(ih_raw.rearrange("p (g c) -> p g c", g=3),
                         a["L0_gnn_w_ih"].rearrange("(g o) c -> o g c", g=3)).then_inc(w_loaded, 16)
            sp.dma_start(hh_raw.rearrange("p (g c) -> p g c", g=3),
                         a["L0_gnn_w_hh"].rearrange("(g o) c -> o g c", g=3)).then_inc(w_loaded, 16)
            sp.dma_start(msg_raw, a["L0_gnn_w_msg"]).then_inc(w_loaded, 16)
            sp.dma_start(rout_raw, a["L0_ffn_router_w"]).then_inc(w_loaded, 16)
            sp.wait_ge(zeroed, 1)
            for r in (0, 32, 64):
                sp.dma_start(se_raw[r:r + 3, :], a["L0_gnn_w_se"]).then_inc(w_loaded, 16)

            def step(q):
                ahead, front = q + 2, q + 1
                if front.exists():
                    wait_quad(sp, adjT_done, front + (-2))
                    load_adj(front)
                if ahead.exists():
                    wait_quad(sp, x_kept, ahead + (-2))
                    wait_quad(sp, xn_ready, ahead + (-2))
                    load_x(ahead)

            run_steps(sp, step)

            for p in range(2):
                sp.wait_ge(scattered[p], 16 * QG * QUADS // 2)
            sp.wait_ge(filled, 16 * FILLS)

            def step(n):
                if n.exists():
                    wait_quad(sp, t_out_ok, n + (-4))
                    sp.dma_start(rows_in[:, n.lap, :, :], groups_v[bass.ds(n.index(), 1)][0]
                                 ).then_inc(rows_loaded[n.lap], 16)

            run_groups(sp, step)

        @block.gpsimd
        def _(pool):
            done_ops = [0]

            def link(ins):
                done_ops[0] += 1
                ins.then_inc(pool_setup, 1)
                pool.wait_ge(pool_setup, done_ops[0])

            def rstd_and_normalize(q, k, nv, rstd_ok, src, dst, done):
                p = q.par
                wait_quad(pool, nv, q)
                pool.tensor_tensor(rstd[:, k + p, :], veps[:, k + p, :], minus_half[:], ALU.pow
                                   ).then_inc(rstd_ok, 1)
                pass_quad(pool, rstd_ok, q, pool_passed)
                for g in range(QG):
                    last = pool.tensor_scalar(dst[:, p, g, :], src[:, p, g, :], negm[:, k + p, g:g + 1],
                                              rstd[:, k + p, g:g + 1], ALU.add, ALU.mult)
                last.then_inc(done, 1)

            link(pool.memset(se_raw, 0.0))
            pool.sem_inc(zeroed, 1)
            pool.dma_start(bmsg[:], a["L0_gnn_b_msg"].rearrange("(o d) -> o d", o=1).to_broadcast([128, D])
                           ).then_inc(bm_loaded, 16)
            link(pool.memset(ident[:], 0.0))
            link(pool.affine_select(out=ident[:], in_=ident[:], compare_op=ALU.not_equal, fill=1.0, base=0,
                                    pattern=[[-1, 128]], channel_multiplier=1))
            link(pool.memset(minus_half[:], -0.5))
            link(pool.memset(ones_bf[:], 1.0))
            rstd_and_normalize(Quad(0), 0, ln1_nv, ln1_rstd, x_nat, xn, xn_ready)
            pool.wait_ge(bn_vec, 1)
            link(pool.tensor_tensor(vec[:, V_V1:V_V1 + 1], vec[:, V_V1:V_V1 + 1], minus_half[:, 0:1], ALU.pow))
            pool.tensor_tensor(vec[:, V_V2:V_V2 + 1], vec[:, V_V2:V_V2 + 1], minus_half[:, 0:1], ALU.pow
                               ).then_inc(bn_pow, 1)
            pool.wait_ge(bn_pow, 1)
            for r in (0, 32, 64):
                pool.dma_start(bse[r:r + 3, :], a["L0_gnn_b_se"].rearrange("(p o) -> p o", o=1)
                               ).then_inc(v_loaded, 16)
            pool.dma_start(brout[:], a["L0_ffn_router_b"].rearrange("(o e) -> o e", o=1)
                           .to_broadcast([128, EXPERTS])).then_inc(v_loaded, 16)
            pool.dma_start(b1_nat[:], a["L0_ffn_b1"]).then_inc(v_loaded, 16)

            def routing_setup():
                link(pool.memset(w1b1[:].rearrange("p e h -> p (e h)"), 0.0))
                pool.sem_inc(zeroed, 1)
                link(pool.affine_select(out=earlier[:], in_=ones_bf[:], compare_op=ALU.is_gt, fill=0.0, base=0,
                                        pattern=[[1, 128]], channel_multiplier=-1))
                for dst, pattern, base, per_row in ((rank[:], [[-1, EXPERTS]], EXPERTS, 0),
                                                    (expert_no[:], [[1, EXPERTS]], 0, 0),
                                                    (bounds[:], [[TILE, TOK // TILE]], 0, 0),
                                                    (token[:], [[NODES, QG]], -TOK, 1),
                                                    (tile_start[:], [[128 * TILE, HALVES]], 0, TILE)):
                    part = ints[:, 0:dst.shape[1]]
                    link(pool.iota(part, pattern=pattern, base=base, channel_multiplier=per_row))
                    link(pool.tensor_copy(dst, part))
                for state in (free, end, opened, has_tile, run):
                    link(pool.memset(state[:], 0.0))
                link(pool.memset(row[:, 0:2, :, R_ID:ROW], 0.0))
                link(pool.memset(t_hid[HID:HID + 1, :, :], 1.0))
                pool.sem_inc(state_zero, 1)

            def step(q):
                front, back, old = q + 1, q + (-1), q + (-2)
                if q.n == 0 and q.it is None:
                    routing_setup()
                p = front.par
                if front.exists() and q.exists():
                    wait_quad(pool, xnT_done, front + (-2))
                    rstd_and_normalize(front, 0, ln1_nv, ln1_rstd, x_nat, xn, xn_ready)
                if back.exists():
                    rstd_and_normalize(back, 2, ln2_nv, ln2_rstd, row[:, :, :, R_X:R_X + D],
                                       row[:, :, :, R_N:R_N + D], yn_ready)
                if front.exists():
                    wait_quad(pool, xnT_hi_ok, front)
                    pool.tensor_tensor(xnT_lo[:, p, :], xnT[:, p, :], f(xnT_hi[:, p, :]), ALU.subtract
                                       ).then_inc(xnT_lo_ok, 1)
                if old.exists():
                    if old.n == 0 and old.it is None:
                        pool.wait_ge(filled, 16 * FILLS)
                    pass_quad(pool, slots_ok, old, pool_passed)
                    for g in range(QG):
                        pool.indirect_dma_start(
                            out=sorted_rows[:, :],
                            out_offset=bass.IndirectOffsetOnAxis(ap=slot[:, old.par, g:g + 1].bitcast(u32), axis=0),
                            in_=row[:, old.par, g, :], in_offset=None, bounds_check=TILES * TILE - 1,
                            oob_is_err=False).then_inc(scattered[old.par], 16)
                if front.exists():
                    wait_quad(pool, h1_hi_ok, front)
                    pool.tensor_tensor(h1_lo[:, p, :, PAD:PAD + NODES], by_graph(h1[:, p, :]),
                                       f(h1_hi[:, p, :, PAD:PAD + NODES]), ALU.subtract).then_inc(h1_lo_ok, 1)
                if q.exists():
                    wait_quad(pool, n_ok, q)
                    pool.tensor_tensor(work[:, DE, :], xnT[:, q.par, :], work[:, N_, :], ALU.subtract
                                       ).then_inc(gru_d, 1)
                if front.exists():
                    wait_quad(pool, exp_ok, front)
                    wait_quad(pool, adjT_ok, front)
                    wait_quad(pool, nmp_done, front + (-2))
                    pool.tensor_tensor(att[:, p, :], work[:, E_, :], adjT[:, p, :], ALU.mult
                                       ).then_inc(att_ok, 1)

            run_steps(pool, step)

            def step(n):
                done = n + (-2)
                if done.exists():
                    pass_quad(pool, t_out_ok, done, pool_passed)
                    for t in range(TG):
                        pool.indirect_dma_start(
                            out=out_rows[:, :],
                            out_offset=bass.IndirectOffsetOnAxis(
                                ap=ids[:, done.lap, t:t + 1].bitcast(u32), axis=0),
                            in_=t_out[:, done.par, t, :], in_offset=None, bounds_check=TOKENS - 1,
                            oob_is_err=False).then_inc(t_scattered[done.lap], 16)

            run_groups(pool, step)
            for lap in range(4):
                pool.wait_ge(t_scattered[lap], 16 * TG * GROUPS // 4)

        @block.scalar
        def _(act):
            for col, name in ((V_V1, "bn1_v"), (V_V2, "bn2_v"), (V_G1, "bn1_g"), (V_G2, "bn2_g"),
                              (V_B1, "bn1_b"), (V_M1, "bn1_m"), (V_B2, "bn2_b"), (V_M2, "bn2_m")):
                act.dma_start(vec[:, col:col + 1], a["L0_gnn_" + name].rearrange("(p o) -> p o", o=1)
                              ).then_inc(bn_loaded, 16)
            for col, name in ((V_IHR, "b_ih"), (V_HHR, "b_hh")):
                for g in range(3):
                    act.dma_start(vec[:, col + g:col + g + 1],
                                  a["L0_gnn_" + name][g * 128:g * 128 + 128].rearrange("(p o) -> p o", o=1)
                                  ).then_inc(b_loaded, 16)
            for n, g in enumerate(BANKS):
                act.wait_ge(w_turned, n + 1)
                lo, hi = g * 512, min(g * 512 + 512, WT_COLS)
                if g == W_SMALL // 4:
                    act.activation(wrout[:], bank[g][:, SE_ROWS:SE_ROWS + EXPERTS], ACT.Copy)
                if g == W_MSG // 4:
                    k = (W_MSG % 4) * 128
                    act.activation(wmsg[:], bank[g][:, k:k + 128], ACT.Copy)
                act.activation(wt_hi[:, lo:hi], bank[g][:, 0:hi - lo], ACT.Copy).then_inc(w_hi, 1)
            act.wait_ge(v_loaded, 16 * SMALL_ONES)
            act.wait_ge(bn_vec, 2)
            act.wait_ge(padded, 1)
            act.wait_ge(template, 1)

            def fill(parts):
                per = TILES // FILLS
                for n in parts:
                    act.dma_start(sorted_rows[n * per * TILE:(n + 1) * per * TILE, :]
                                  .rearrange("(t p) c -> p t c", p=TILE),
                                  fill_row.rearrange("p (o c) -> p o c", o=1).to_broadcast([128, per, ROW])
                                  ).then_inc(filled, 16)

            def step(q):
                front, back = q + 1, q + (-1)
                if q.it is None and 0 <= q.n < 2:
                    fill(range(q.n * FILLS // 2, (q.n + 1) * FILLS // 2))
                if q.it is None and q.n == 2:
                    act.wait_ge(b1_placed, 1)
                    act.dma_start(w1b1[:, :, 0:HID], a["L0_ffn_W1"].rearrange("e d h -> d e h")
                                  ).then_inc(e_loaded, 16)
                    act.dma_start(w2b2[0:HID, :].rearrange("p (e d) -> p e d", e=EXPERTS),
                                  a["L0_ffn_W2"].rearrange("e h d -> h e d")).then_inc(e_loaded, 16)
                    act.dma_start(w2b2[HID:HID + 1, :], a["L0_ffn_b2"].rearrange("(o e) d -> o (e d)", o=1)
                                  ).then_inc(e_loaded, 16)
                if q.exists():
                    wait_quad(act, nmp_done, q)
                    wait_quad(act, gate_n_i, q + (-2))
                    act.activation(nmp_hi[:, q.par, :], bank[2][:], ACT.Copy).then_inc(nmp_hi_ok, 1)
                if front.exists():
                    p = front.par
                    wait_dma(act, x_loaded, front)
                    wait_quad(act, x2_ok, front + (-2))
                    act.activation(x_keep[:, p, :, :], x_nat[:, p, :, :], ACT.Copy).then_inc(x_kept, 1)
                    wait_quad(act, xnT_done, front)
                    wait_quad(act, gru_d, front + (-2))
                    act.activation(xnT[:, p, :], bank[2][:], ACT.Copy).then_inc(xnT_full, 1)
                    wait_quad(act, adjT_done, front)
                    wait_quad(act, att_ok, front + (-2))
                    act.activation(adjT[:, p, :], bank[3][:], ACT.Copy).then_inc(adjT_ok, 1)
                if q.exists():
                    wait_quad(act, xc_t, q)
                    wait_quad(act, gate_n_i, q + (-2))
                    act.activation(xc_hi[:, q.par, :], work[:, T_, :], ACT.Relu).then_inc(xc_hi_ok, 1)
                if back.exists():
                    wait_quad(act, ynT_done, back)
                    wait_quad(act, logit_done, back + (-1))
                    act.activation(ynT[:], bank[1][:], ACT.Copy).then_inc(ynT_ok, 1)
                if q.exists():
                    wait_quad(act, gate_n_h, q)
                    wait_quad(act, rgh_ok, q + (-1))
                    act.activation(work[:, GH, :], bank[7][:], ACT.Identity, bias=vec[:, V_HN:V_HN + 1],
                                   scale=0.5).then_inc(gh_ok, 1)
                if front.exists():
                    wait_quad(act, conv1_done, front)
                    wait_quad(act, h1_lo_ok, front + (-2))
                    act.activation(h1[:, p, :], bank[2][:], ACT.Relu, bias=vec[:, V_T1:V_T1 + 1]
                                   ).then_inc(h1_full, 1)
                    wait_quad(act, se_done, front)
                    wait_quad(act, dist_done, front + (-2))
                    act.activation(dist_r[0:3, p, :], bank[3][0:3, :], ACT.Identity, bias=bse[0:3, :])
                    act.activation(dist_r[32:35, p, :], bank[3][32:35, :], ACT.Square, bias=bse[32:35, :])
                    act.activation(dist_l[64:67, p, :], bank[3][64:67, :], ACT.Square, bias=bse[64:67, :]
                                   ).then_inc(se_sq, 1)
                if q.exists():
                    wait_quad(act, gate_r, q)
                    act.activation(work[:, TR, :], bank[4][:], ACT.Tanh, bias=vec[:, V_HR:V_HR + 1],
                                   scale=0.5).then_inc(tr_ok, 1)
                    wait_quad(act, gate_z, q)
                    wait_quad(act, gru_e, q + (-1))
                    act.activation(work[:, TZ, :], bank[5][:], ACT.Tanh, bias=vec[:, V_HZ:V_HZ + 1],
                                   scale=0.5).then_inc(tz_ok, 1)
                    wait_quad(act, w_ok, q)
                    wait_quad(act, gru_f, q + (-1))
                    act.activation(work[:, N_, :], work[:, W_, :], ACT.Tanh, bias=vec[:, V_IHN:V_IHN + 1]
                                   ).then_inc(n_ok, 1)
                if front.exists():
                    wait_quad(act, dist_done, front)
                    wait_quad(act, att_ok, front + (-1))
                    act.activation(work[:, E_, :], bank[2][:], ACT.Exp, scale=2.0).then_inc(exp_ok, 1)
                    wait_quad(act, msg_sum, front)
                    act.activation(msg[:, p, :], msg[:, p, :], ACT.Relu).then_inc(msg_ok, 1)

            run_steps(act, step)

            def step(n):
                before = n + (-1)
                if n.exists():
                    wait_quad(act, t_turned, n)
                    wait_quad(act, t_hid_done, n + (-2))
                    act.activation(t_ynT[:, n.par, :], bank[n.par][:], ACT.Copy).then_inc(t_ynT_ok, 1)
                if before.exists():
                    p = before.par
                    wait_quad(act, t_hid_done, before)
                    wait_quad(act, t_out_done, before + (-2))
                    for t in range(TG):
                        cols = slice(t * 128, t * 128 + 128)
                        last = act.activation(t_hid[0:HID, p, cols], bank[2 + p][0:HID, cols], ACT.Relu,
                                              bias=t_w1[0:HID, p, t, HID:HID + 1])
                    last.then_inc(t_hid_ok, 1)

            run_groups(act, step)

        @block.vector
        def _(dve):
            chain = [0]

            def link(ins):
                chain[0] += 1
                ins.then_inc(dve_setup, 1)
                dve.wait_ge(dve_setup, chain[0])

            def layer_stats(q, k, src, stats_ok, mv_ok, nv_ok):
                p = q.par
                for g in range(QG):
                    last = dve.bn_stats(stats[:, p, g, :], src[:, p, g, :])
                last.then_inc(stats_ok, 1)
                pass_quad(dve, stats_ok, q, dve_passed)
                for g in range(QG):
                    last = dve.bn_aggr(mv[:, p, g, :], stats[:, p, g, :])
                last.then_inc(mv_ok, 1)
                wait_quad(dve, mv_ok, q)
                dve.tensor_scalar(negm[:, k + p, :], mv[:, p, :, 0], -1.0, None, ALU.mult)
                dve.tensor_scalar(veps[:, k + p, :], mv[:, p, :, 1], EPS, None, ALU.add).then_inc(nv_ok, 1)

            link(dve.memset(fill_row, 0.0))
            link(dve.memset(fill_row[:, R_ID:R_ID + 1].bitcast(i32), NO_TOKEN))
            dve.sem_inc(template, 1)
            wait_dma(dve, x_loaded, Quad(0))
            layer_stats(Quad(0), 0, x_nat, ln1_stats, ln1_mv, ln1_nv)
            for part in (h1_hi, h1_lo):
                graphs = f(part[:]).rearrange("p a g n -> p (a g) n")
                dve.memset(graphs[:, :, 0:PAD], 0.0)
                dve.memset(graphs[:, :, PAD + NODES:PADDED], 0.0)
            link(dve.memset(dist_l[:], 0.0))
            link(dve.memset(dist_r[:], 0.0))
            link(dve.memset(dist_l[32:35, :, :], -0.5))
            link(dve.memset(dist_r[64:67, :, :], -0.5))
            dve.sem_inc(padded, 1)
            dve.wait_ge(bn_loaded, 16 * BN_VECTORS)
            dve.tensor_scalar(vec[:, V_V1:V_V1 + 1], vec[:, V_V1:V_V1 + 1], EPS, None, ALU.add)
            dve.tensor_scalar(vec[:, V_V2:V_V2 + 1], vec[:, V_V2:V_V2 + 1], EPS, None, ALU.add).then_inc(bn_vec, 1)
            dve.wait_ge(bn_pow, 1)
            for s, g, v, m, b, t in ((V_S1, V_G1, V_V1, V_M1, V_B1, V_T1), (V_S2, V_G2, V_V2, V_M2, V_B2, V_T2)):
                link(dve.tensor_tensor(vec[:, s:s + 1], vec[:, g:g + 1], vec[:, v:v + 1], ALU.mult))
                link(dve.tensor_tensor(vec[:, t:t + 1], vec[:, m:m + 1], vec[:, s:s + 1], ALU.mult))
                link(dve.tensor_tensor(vec[:, t:t + 1], vec[:, b:b + 1], vec[:, t:t + 1], ALU.subtract))
            dve.wait_ge(w_loaded, 16 * 9)
            dve.tensor_scalar(c1_raw, c1_raw, vec[:, V_S1:V_S1 + 1], None, ALU.mult)
            dve.tensor_scalar(c2_raw, c2_raw, vec[:, V_S2:V_S2 + 1], None, ALU.mult).then_inc(bn_scaled, 1)
            dve.wait_ge(b_loaded, 16 * BIASES)
            link(dve.tensor_tensor(vec[:, V_HR:V_HR + 2], vec[:, V_IHR:V_IHR + 2], vec[:, V_HHR:V_HHR + 2], ALU.add))
            dve.tensor_scalar(vec[:, V_HR:V_HR + 2], vec[:, V_HR:V_HR + 2], 0.5, None, ALU.mult)
            dve.tensor_scalar(vec[:, V_HN:V_HN + 1], vec[:, V_HHN:V_HHN + 1], 0.5, None, ALU.mult
                              ).then_inc(bn_vec, 1)
            for n, g in enumerate(BANKS):
                dve.wait_ge(w_hi, n + 1)
                lo, hi = g * 512, min(g * 512 + 512, WT_COLS)
                dve.tensor_tensor(wt_lo[:, lo:hi], bank[g][:, 0:hi - lo], f(wt_hi[:, lo:hi]), ALU.subtract
                                  ).then_inc(w_lo, 1)

            def then(q, k, ins):
                ins.then_inc(route[k], 1)
                wait_quad(dve, route[k], q)

            counts = ranked_counts[:, QG * EXPERTS:(QG + 1) * EXPERTS]
            ranks = by_graph(ranked_counts[:, 0:QG * EXPERTS])

            def open_tiles(q):
                wait_quad(dve, counted, q)
                dve.tensor_copy(ranked_counts[:], bank[1][:, 0:(QG + 1) * EXPERTS]).then_inc(ranks_kept, 1)
                wait_quad(dve, ranks_kept, q)
                then(q, 0, dve.tensor_tensor(over[:], counts, free[:], ALU.subtract))
                dve.tensor_scalar(opens[:], over[:], 0.0, None, ALU.is_gt)
                then(q, 1, dve.tensor_tensor(past[:], over_graphs(over[:]), bounds[:].rearrange(
                    "p (g o) -> p g o", o=1).to_broadcast([128, TOK // TILE, EXPERTS]), ALU.is_gt))
                dve.tensor_tensor(in_open[:], ranks, over_graphs(free[:]), ALU.is_lt)
                then(q, 2, dve.tensor_reduce(new_base[:], past[:].rearrange("p k e -> p e k"), AX.X, ALU.add))
                dve.tensor_scalar(news[:], new_base[:], float(TILE), None, ALU.mult)
                then(q, 3, dve.tensor_scalar(run[:, 0, SHIFT:], new_base[:], float(TILE), None, ALU.mult))
                at = 0
                for k in range(5):
                    then(q, 4 + k, dve.tensor_tensor(run[:, 1 - at, SHIFT:], run[:, at, SHIFT:],
                                                     run[:, at, SHIFT - (1 << k):SHIFT + EXPERTS - (1 << k)],
                                                     ALU.add))
                    at = 1 - at
                then(q, 9, dve.tensor_scalar(new_end[:], run[:, at, SHIFT:], opened[:], None, ALU.add))

            def give_slots(q):
                dve.tensor_copy(opened[:], new_end[:, EXPERTS - 1:EXPERTS])
                dve.tensor_tensor(run[:, 0, SHIFT:], new_end[:], end[:], ALU.subtract)
                then(q, 10, dve.tensor_tensor(new_base[:], new_end[:], news[:], ALU.subtract))
                dve.tensor_tensor(off_new[:], new_base[:], free[:], ALU.subtract)
                dve.tensor_tensor(off_open[:], end[:], new_base[:], ALU.subtract)
                for h in range(HALVES):
                    last = dve.tensor_scalar(tile_cmp[:, h, :], new_base[:], tile_start[:, h:h + 1], None,
                                             ALU.is_le)
                then(q, 11, last)
                dve.tensor_tensor(in_open[:], in_open[:], over_graphs(off_open[:]), ALU.mult)
                dve.tensor_tensor(slot_e[:], ranks, over_graphs(off_new[:]), ALU.add)
                dve.tensor_tensor(run[:, 0, SHIFT:], run[:, 0, SHIFT:], opens[:], ALU.mult)
                dve.tensor_tensor(free[:], news[:], over[:], ALU.subtract)
                dve.tensor_scalar(token[:], token[:], float(TOK), None, ALU.add)
                for h in range(HALVES):
                    last = dve.scalar_tensor_tensor(out=tile_cmp[:, h, :], in0=new_end[:],
                                                    scalar=tile_start[:, h:h + 1], in1=tile_cmp[:, h, :],
                                                    op0=ALU.is_gt, op1=ALU.mult)
                then(q, 12, last)
                dve.tensor_tensor(slot_e[:], slot_e[:], in_open[:], ALU.add)
                dve.tensor_tensor(end[:], end[:], run[:, 0, SHIFT:], ALU.add)
                wait_scatter(dve, q + (-2))
                dve.tensor_copy(row[:, q.par, :, R_ID].bitcast(i32), token[:])
                then(q, 13, dve.tensor_tensor(has_tile[:], has_tile[:], tile_cmp[:], ALU.add))
                then(q, 14, dve.tensor_tensor(slot_e[:], slot_e[:], onehot[:], ALU.mult))
                then(q, 15, dve.tensor_reduce(slot_f[:], slot_e[:], AX.X, ALU.add))
                dve.tensor_copy(slot[:, q.par, :], slot_f[:]).then_inc(slots_ok, 1)

            def step(q):
                ahead, front, back, old = q + 2, q + 1, q + (-1), q + (-2)
                if q.n == 1 and q.it is None:
                    dve.wait_ge(v_loaded, 16 * SMALL_ONES)
                    link(dve.transpose(b1_turned[:], b1_nat[:]))
                    dve.wait_ge(zeroed, 2)
                    link(dve.tensor_copy(w1b1[0:HID, :, HID], b1_turned[:]))
                    dve.sem_inc(b1_placed, 1)
                if q.n == 2 and q.it is None:
                    dve.wait_ge(state_zero, 1)
                if old.exists():
                    open_tiles(old)
                if back.exists():
                    wait_quad(dve, gruT_done, back)
                    wait_scatter(dve, back + (-2))
                    dve.tensor_tensor(row[:, back.par, :, R_X:R_X + D], by_graph(bank[3][:]),
                                      x_keep[:, back.par, :, :], ALU.add).then_inc(x2_ok, 1)
                if q.exists():
                    wait_quad(dve, nmp_hi_ok, q)
                    dve.tensor_tensor(nmp_lo[:, q.par, :], bank[2][:], f(nmp_hi[:, q.par, :]),
                                      ALU.subtract).then_inc(nmp_lo_ok, 1)
                if back.exists():
                    wait_quad(dve, x2_ok, back)
                    layer_stats(back, 2, row[:, :, :, R_X:R_X + D], ln2_stats, ln2_mv, ln2_nv)
                if old.exists():
                    give_slots(old)
                if q.exists():
                    wait_quad(dve, conv2_done, q)
                    dve.scalar_tensor_tensor(out=work[:, T_, :], in0=bank[0][:], scalar=vec[:, V_T2:V_T2 + 1],
                                             in1=xnT[:, q.par, :], op0=ALU.add, op1=ALU.add).then_inc(xc_t, 1)
                if front.exists():
                    p = front.par
                    wait_quad(dve, xnT_full, front)
                    wait_quad(dve, gate_n_i, front + (-2))
                    dve.tensor_copy(xnT_hi[:, p, :], xnT[:, p, :]).then_inc(xnT_hi_ok, 1)
                if q.exists():
                    wait_quad(dve, xc_hi_ok, q)
                    dve.scalar_tensor_tensor(out=xc_lo[:, q.par, :], in0=work[:, T_, :], scalar=0.0,
                                             in1=f(xc_hi[:, q.par, :]), op0=ALU.max, op1=ALU.subtract
                                             ).then_inc(xc_lo_ok, 1)
                if ahead.exists():
                    wait_dma(dve, x_loaded, ahead)
                    layer_stats(ahead, 0, x_nat, ln1_stats, ln1_mv, ln1_nv)
                if front.exists():
                    wait_quad(dve, h1_full, front)
                    wait_quad(dve, conv2_done, front + (-2))
                    dve.tensor_copy(h1_hi[:, p, :, PAD:PAD + NODES], by_graph(h1[:, p, :])).then_inc(h1_hi_ok, 1)
                    wait_quad(dve, se_sq, front)
                    dve.tensor_copy(dist_l[0:3, p, :], dist_r[0:3, p, :]).then_inc(se_l, 1)
                if q.exists():
                    wait_quad(dve, tr_ok, q)
                    wait_quad(dve, gh_ok, q)
                    dve.scalar_tensor_tensor(out=work[:, W_, :], in0=work[:, TR, :], scalar=1.0,
                                             in1=work[:, GH, :], op0=ALU.add, op1=ALU.mult).then_inc(rgh_ok, 1)
                    wait_quad(dve, rgh_ok, q)
                    wait_quad(dve, gate_n_i, q)
                    dve.tensor_tensor(work[:, W_, :], bank[6][:], work[:, W_, :], ALU.add).then_inc(w_ok, 1)
                if back.exists():
                    wait_quad(dve, logit_done, back)
                    dve.tensor_tensor(logits[:], by_graph(bank[1][:, 0:QG * EXPERTS]), over_graphs(brout[:]),
                                      ALU.add).then_inc(logits_ok, 1)
                    wait_quad(dve, logits_ok, back)
                    dve.tensor_reduce(lmax[:], logits[:], AX.X, ALU.max).then_inc(am_max, 1)
                    wait_quad(dve, am_max, back)
                    dve.tensor_tensor(ranked[:], logits[:], lmax[:].rearrange("p (g o) -> p g o", o=1)
                                      .to_broadcast([128, QG, EXPERTS]), ALU.is_equal).then_inc(am_eq, 1)
                    wait_quad(dve, am_eq, back)
                    dve.tensor_tensor(ranked[:], ranked[:], over_graphs(rank[:]), ALU.mult).then_inc(am_rank, 1)
                    wait_quad(dve, am_rank, back)
                    dve.tensor_reduce(first[:], ranked[:], AX.X, ALU.max).then_inc(am_first, 1)
                    wait_quad(dve, am_first, back)
                    dve.tensor_tensor(onehot[:], ranked[:], first[:].rearrange("p (g o) -> p g o", o=1)
                                      .to_broadcast([128, QG, EXPERTS]), ALU.is_equal).then_inc(onehot_ok, 1)
                if front.exists():
                    if front.n == 0 and front.it is None:
                        dve.wait_ge(bm_loaded, 16)
                    wait_quad(dve, msg_done, front)
                    wait_quad(dve, nmp_done, front + (-2))
                    dve.tensor_tensor(by_graph(msg[:, p, :]), by_graph(bank[3][:]),
                                      bmsg[:].rearrange("p (o d) -> p o d", o=1).to_broadcast([128, QG, D]),
                                      ALU.add).then_inc(msg_sum, 1)
                if q.exists():
                    wait_quad(dve, gru_d, q)
                    wait_quad(dve, tz_ok, q)
                    dve.scalar_tensor_tensor(out=work[:, DE, :], in0=work[:, TZ, :], scalar=1.0,
                                             in1=work[:, DE, :], op0=ALU.add, op1=ALU.mult).then_inc(gru_e, 1)
                    wait_quad(dve, gru_e, q)
                    wait_quad(dve, gruT_done, q + (-1))
                    dve.scalar_tensor_tensor(out=work[:, F_, :], in0=work[:, DE, :], scalar=0.5,
                                             in1=work[:, N_, :], op0=ALU.mult, op1=ALU.add).then_inc(gru_f, 1)

            run_steps(dve, step)

            last_quad = Quad(QUADS - 1)
            wait_quad(dve, slots_ok, last_quad)
            dve.tensor_tensor(tile_cmp[:], has_tile[:], expert_no[:].rearrange("p (o e) -> p o e", o=1)
                              .to_broadcast([128, HALVES, EXPERTS]), ALU.mult).then_inc(table_sum, 1)
            dve.wait_ge(table_sum, 1)
            dve.tensor_reduce(tile_e[:], tile_cmp[:], AX.X, ALU.add).then_inc(table_sum, 1)
            dve.wait_ge(table_row, 1)
            dve.tensor_copy(tile_expert[:], bank[0][0:1, 0:HALVES * 128]).then_inc(table_ok, 1)
            dve.wait_ge(table_ok, 1)
            dve.wait_ge(e_loaded, 48)

            dve_regs = [dve.alloc_register(f"dve_expert{t}") for t in range(TG)]

            def step(n):
                done = n + (-2)
                if n.exists():
                    p = n.par
                    pass_quad(dve, t_hid_ok, n + (-2), dve_passed)
                    experts = experts_of(dve, dve_regs, n)
                    for t, e in enumerate(experts):
                        last = dve.tensor_copy(t_w1[:, p, t, :],
                                               w1b1[:, bass.ds(e, 1), :].rearrange("p o h -> p (o h)"))
                    last.then_inc(t_w1_ok, 1)
                if done.exists():
                    p = done.par
                    wait_quad(dve, t_out_done, done)
                    wait_tiles_scattered(dve, done + (-2))
                    dve.tensor_copy(ids[:, done.lap, :], rows_in[:, done.lap, :, R_ID].bitcast(i32))
                    dve.scalar_tensor_tensor(out=t_out[:, p, :, :], in0=by_graph(bank[4 + p][:]), scalar=0.0,
                                             in1=rows_in[:, done.lap, :, R_X:R_X + D], op0=ALU.max, op1=ALU.add
                                             ).then_inc(t_out_ok, 1)

            run_groups(dve, step)

        @block.tensor
        def _(pe):
            def raw(i):
                if i < TAPS:
                    return c2_raw.rearrange("p (i k) -> p i k", k=TAPS)[:, :, i]
                if i == W_CONV1:
                    return c1_raw
                if i < W_IH_NMP:
                    return ih_raw[:, (i - W_IH_CONV) * 256:(i - W_IH_CONV) * 256 + 128]
                if i < W_HH:
                    return ih_raw[:, (i - W_IH_NMP) * 256 + 128:(i - W_IH_NMP) * 256 + 256]
                if i < W_MSG:
                    return hh_raw[:, (i - W_HH) * 128:(i - W_HH) * 128 + 128]
                return msg_raw

            pe.wait_ge(pool_setup, 5)
            pe.wait_ge(w_loaded, 16 * 9)
            for g in BANKS:
                if g == 7:
                    pe.transpose(bank[7][:, 0:SE_ROWS], se_raw, ident[0:SE_ROWS, 0:SE_ROWS])
                    last = pe.transpose(bank[7][:, SE_ROWS:SE_ROWS + EXPERTS], rout_raw,
                                        ident[0:EXPERTS, 0:EXPERTS])
                else:
                    if g == W_CONV1 // 4:
                        pe.wait_ge(bn_scaled, 1)
                    for k in range(4):
                        last = pe.transpose(bank[g][:, k * 128:k * 128 + 128], raw(4 * g + k), ident[:])
                last.then_inc(w_turned, 1)
            pe.wait_ge(w_lo, BANKS.index(3) + 1)

            def split3(dst, lo_col, cols, hi, lo, start, stop):
                wh, wl = wt_hi[:, lo_col:lo_col + cols], wt_lo[:, lo_col:lo_col + cols]
                pe.matmul(dst, wh, hi, start=start, stop=False)
                pe.matmul(dst, wh, lo, start=False, stop=False)
                return pe.matmul(dst, wl, hi, start=False, stop=stop)

            def block_of(i, dst, hi, lo, start, stop):
                return split3(dst, i * 128, 128, hi, lo, start, stop)

            def turn(dst, src):
                for g in range(QG):
                    last = pe.transpose(dst[:, g * 128:g * 128 + 128], src(g), ident[:])
                return last

            def conv2(q, taps):
                for k in taps:
                    last = block_of(W_CONV2 + k, bank[0][:], h1_hi[:, q.par, :, k:k + NODES],
                                    h1_lo[:, q.par, :, k:k + NODES], k == 0, k == TAPS - 1)
                return last

            def step(q):
                front, back, old = q + 1, q + (-1), q + (-2)
                if q.n == 0 and q.it is None:
                    pe.wait_ge(w_lo, 8)
                if q.exists():
                    wait_quad(pe, h1_hi_ok, q)
                    wait_quad(pe, h1_lo_ok, q)
                    wait_quad(pe, xc_t, back)
                    conv2(q, range(0, 2))
                if old.exists():
                    if old.n == 0 and old.it is None:
                        pe.wait_ge(state_zero, 1)
                    wait_quad(pe, onehot_ok, old)
                    def blocks(first, end):
                        return bank[1][:, first * EXPERTS:end * EXPERTS].rearrange("p (g e) -> p g e",
                                                                                  g=end - first)

                    def graph(g, times):
                        return onehot[:, g:g + 1, :].to_broadcast([128, times, EXPERTS])

                    pe.matmul(blocks(0, 1), earlier[:], onehot[:, 0:1, :], start=True, stop=True)
                    pe.matmul(blocks(1, QG + 1), ones_bf[:], graph(0, QG), start=True, stop=False)
                    pe.matmul(blocks(1, QG), earlier[:], onehot[:, 1:QG, :], start=False, stop=False)
                    for g in range(1, QG):
                        last = pe.matmul(blocks(g + 1, QG + 1), ones_bf[:], graph(g, QG - g), start=False,
                                         stop=g == QG - 1)
                    last.then_inc(counted, 1)
                if q.exists():
                    conv2(q, range(2, 5))
                    wait_quad(pe, exp_ok, q)
                    wait_quad(pe, msg_ok, q)
                    wait_quad(pe, att_ok, q)
                    for g in range(QG):
                        cols = slice(g * 128, g * 128 + 128)
                        last = pe.matmul(bank[2][:, cols], msg[:, q.par, cols], att[:, q.par, cols],
                                         start=True, stop=True)
                    last.then_inc(nmp_done, 1)
                if back.exists():
                    wait_quad(pe, gru_f, back)
                    if q.exists():
                        wait_quad(pe, msg_sum, q)
                    turn(bank[3], lambda g: work[:, F_, g * 128:g * 128 + 128]).then_inc(gruT_done, 1)
                if q.exists():
                    conv2(q, range(5, TAPS)).then_inc(conv2_done, 1)
                if front.exists():
                    p = front.par
                    wait_quad(pe, xn_ready, front)
                    if q.exists():
                        wait_quad(pe, nmp_lo_ok, q)
                    turn(bank[2], lambda g: xn[:, p, g, :]).then_inc(xnT_done, 1)
                    wait_dma(pe, adj_loaded, front)
                    if back.exists():
                        wait_quad(pe, x2_ok, back)
                    turn(bank[3], lambda g: adj_nat[:, p, g, :]).then_inc(adjT_done, 1)
                if back.exists():
                    wait_quad(pe, yn_ready, back)
                    wait_quad(pe, ranks_kept, old)
                    turn(bank[1], lambda g: row[:, back.par, g, R_N:R_N + D]).then_inc(ynT_done, 1)
                if q.exists():
                    s = q.par
                    wait_quad(pe, w_ok, back)
                    wait_quad(pe, tz_ok, back)
                    xh, xl, nh, nl = xnT_hi[:, s, :], xnT_lo[:, s, :], nmp_hi[:, s, :], nmp_lo[:, s, :]
                    block_of(W_HH + 2, bank[7][:], xh, xl, True, True).then_inc(gate_n_h, 1)
                    wait_quad(pe, nmp_hi_ok, q)
                    wait_quad(pe, nmp_lo_ok, q)
                    for i in range(2):
                        block_of(W_HH + i, bank[4 + i][:], xh, xl, True, False)
                        block_of(W_IH_NMP + i, bank[4 + i][:], nh, nl, False, False)
                    block_of(W_IH_NMP + 2, bank[6][:], nh, nl, True, False)
                if front.exists():
                    wait_quad(pe, xnT_hi_ok, front)
                    wait_quad(pe, xnT_lo_ok, front)
                    block_of(W_CONV1, bank[2][:], xnT_hi[:, p, :], xnT_lo[:, p, :], True, True
                             ).then_inc(conv1_done, 1)
                    wait_quad(pe, adjT_ok, front)
                    split3(bank[3][0:SE_ROWS, :], SE_COL, SE_ROWS, xnT_hi[:, p, :], xnT_lo[:, p, :], True, True
                           ).then_inc(se_done, 1)
                if back.exists():
                    wait_quad(pe, ynT_ok, back)
                    for g in range(QG):
                        last = pe.matmul(bank[1][:, g * EXPERTS:(g + 1) * EXPERTS], ynT[:, g * 128:g * 128 + 128],
                                         wrout[:], start=True, stop=True)
                    last.then_inc(logit_done, 1)
                if q.exists():
                    wait_quad(pe, xc_hi_ok, q)
                    wait_quad(pe, xc_lo_ok, q)
                    for i, done in enumerate((gate_r, gate_z, gate_n_i)):
                        block_of(W_IH_CONV + i, bank[4 + i][:], xc_hi[:, s, :], xc_lo[:, s, :], False, True
                                 ).then_inc(done, 1)
                if front.exists():
                    wait_quad(pe, h1_full, front)
                    wait_quad(pe, se_sq, front)
                    wait_quad(pe, se_l, front)
                    for g in range(QG):
                        cols = slice(g * 128, g * 128 + 128)
                        last = pe.matmul(bank[2][:, cols], dist_l[:, p, cols], dist_r[:, p, cols],
                                         start=True, stop=True)
                    last.then_inc(dist_done, 1)
                    for g in range(QG):
                        last = pe.matmul(bank[3][:, g * 128:g * 128 + 128], xnT[:, p, g * 128:g * 128 + 128],
                                         wmsg[:], start=True, stop=True)
                    last.then_inc(msg_done, 1)

            run_steps(pe, step)

            pe.wait_ge(table_sum, 2)
            for h in range(HALVES):
                last = pe.matmul(bank[0][0:1, h * 128:h * 128 + 128], tile_e[:, h:h + 1], ident[:],
                                 start=True, stop=True)
            last.then_inc(table_row, 1)
            pe.wait_ge(table_ok, 1)
            pe.wait_ge(e_loaded, 48)

            pe_regs = [pe.alloc_register(f"pe_expert{t}") for t in range(TG)]

            def step(n):
                before, done = n + (-1), n + (-2)
                if n.exists():
                    wait_dma(pe, rows_loaded, n)
                    wait_quad(pe, t_ynT_ok, n + (-2))
                    turn(bank[n.par], lambda t: rows_in[:, n.lap, t, R_N:R_N + D]).then_inc(t_turned, 1)
                if before.exists():
                    p = before.par
                    wait_quad(pe, t_ynT_ok, before)
                    wait_quad(pe, t_w1_ok, before)
                    wait_quad(pe, t_hid_ok, before + (-2))
                    for t in range(TG):
                        cols = slice(t * 128, t * 128 + 128)
                        last = pe.matmul(bank[2 + p][0:HID, cols], t_w1[:, p, t, 0:HID], t_ynT[:, p, cols],
                                         start=True, stop=True)
                    last.then_inc(t_hid_done, 1)
                if done.exists():
                    p = done.par
                    experts = experts_of(pe, pe_regs, done)
                    wait_quad(pe, t_out_ok, done + (-2))
                    pass_quad(pe, t_hid_ok, done, pe_passed)
                    for t, e in enumerate(experts):
                        last = pe.matmul(bank[4 + p][:, t * 128:t * 128 + 128],
                                         t_hid[:, p, t * 128:t * 128 + 128], w2b2[:, bass.ds(e * D, D)],
                                         start=True, stop=True)
                    last.then_inc(t_out_done, 1)

            run_groups(pe, step)


def kernel(**inputs):
    import concourse.bacc as bacc
    from concourse.bass_utils import run_bass_kernel_spmd

    nc = bacc.Bacc("TRN2", target_bir_lowering=False, num_devices=1)
    arrays, args = {}, {}
    for name, value in inputs.items():
        value = np.ascontiguousarray(value)
        arrays[f"in_{name}"] = value
        args[name] = nc.dram_tensor(f"in_{name}", value.shape, mybir.dt.from_np(value.dtype),
                                    kind="ExternalInput").ap()
    out = nc.dram_tensor("out", (GRAPHS, NODES, D), mybir.dt.float32, kind="ExternalOutput").ap()
    program(nc, args, out)
    result = run_bass_kernel_spmd(nc, [arrays], core_ids=[0])
    return np.asarray(result.results[0]["out"])
```
